# Optimizing a Trainium2 kernel written in Bass

```python
import numpy as np
import jax
import jax.numpy as jnp

def _softmax(x, axis=-1):
    return jax.nn.softmax(x, axis=axis)

def _gelu(x):
    return jax.nn.gelu(x, approximate=True)

def _silu(x):
    return jax.nn.silu(x)

def _sigmoid(x):
    return jax.nn.sigmoid(x)

def _layernorm(x, axis=-1, eps=1e-05):
    m = jnp.mean(x, axis=axis, keepdims=True)
    v = jnp.var(x, axis=axis, keepdims=True)
    return (x - m) / jnp.sqrt(v + eps)

def _scatter_add(tgt, idx, src, axis=0):
    return tgt.at[idx].add(src)

def _segment_sum(src, seg, n):
    return jax.ops.segment_sum(src, seg, n)
kernel_name = 'mk_seq_preln_d1_jaxref_r8_2951e1'

def setup_inputs(seed: int=0):
    np.random.seed(seed)
    _w = jnp.asarray

    def _L0_attn_setup():
        import jax, jax.numpy as jnp
        import numpy as np
        DIM = 128
        HEADS = 16
        DIM_HEAD = 64
        SCALE = 16.0
        EPS = 1e-05

        def layernorm(x, g):
            mean = jnp.mean(x, axis=-1, keepdims=True)
            var = jnp.var(x, axis=-1, keepdims=True)
            return (x - mean) * jax.lax.rsqrt(var + EPS) * g

        def l2norm(t):
            return t / jnp.maximum(jnp.linalg.norm(t, axis=-1, keepdims=True), 1e-12)
        key = jax.random.key(seed)
        ks = jax.random.split(key, 5)
        inner = HEADS * DIM_HEAD
        x = jax.random.normal(ks[0], (2, 256, DIM), dtype=jnp.float32)
        Wq = jax.random.normal(ks[1], (inner, DIM), dtype=jnp.float32) * 0.02
        Wkv = jax.random.normal(ks[2], (2 * DIM_HEAD, DIM), dtype=jnp.float32) * 0.02
        Wout = jax.random.normal(ks[3], (DIM, inner), dtype=jnp.float32) * 0.02
        g1 = jnp.ones((DIM,), dtype=jnp.float32)
        g2 = jnp.ones((DIM,), dtype=jnp.float32)
        return {'x': x, 'g1': g1, 'Wq': Wq, 'Wkv': Wkv, 'Wout': Wout, 'g2': g2}
    _L0_attn_in = _L0_attn_setup()

    def _L0_ffn_setup():
        import jax, jax.numpy as jnp
        import numpy as np
        import math
        N_EXP = 8
        TOP_K = 2
        CAPACITY_FACTOR = 1.25

        def _capacity(num_tokens):
            cap = math.floor(TOP_K * CAPACITY_FACTOR * num_tokens / N_EXP)
            cap += cap % 2
            return int(cap)
        key = jax.random.key(seed)
        k1, k2, k3, k4 = jax.random.split(key, 4)
        B, C, d = (4, 128, 128)
        x = jax.random.normal(k1, (B, C, d), dtype=jnp.float32)
        w_g = jax.random.normal(k2, (d, N_EXP), dtype=jnp.float32) * 0.02
        c_fc = jax.random.normal(k3, (N_EXP, d, 4 * d), dtype=jnp.float32) * 0.02
        c_proj = jax.random.normal(k4, (N_EXP, 4 * d, d), dtype=jnp.float32) * 0.02
        return {'x': x, 'w_g': w_g, 'c_fc': c_fc, 'c_proj': c_proj}
    _L0_ffn_in = _L0_ffn_setup()
    _d = {'L0_attn_x': _L0_attn_in['x'], 'L0_attn_g1': _L0_attn_in['g1'], 'L0_attn_Wq': _L0_attn_in['Wq'], 'L0_attn_Wkv': _L0_attn_in['Wkv'], 'L0_attn_Wout': _L0_attn_in['Wout'], 'L0_attn_g2': _L0_attn_in['g2'], 'L0_ffn_w_g': _L0_ffn_in['w_g'], 'L0_ffn_c_fc': _L0_ffn_in['c_fc'], 'L0_ffn_c_proj': _L0_ffn_in['c_proj']}
    _x0 = _d['L0_attn_x']
    _d['L0_attn_x'] = jax.random.normal(jax.random.fold_in(jax.random.key(seed), 1), (8, 512, 128), dtype=_x0.dtype)
    del _x0
    return _d

def reference(L0_attn_x, L0_attn_g1, L0_attn_Wq, L0_attn_Wkv, L0_attn_Wout, L0_attn_g2, L0_ffn_w_g, L0_ffn_c_fc, L0_ffn_c_proj):

    def _L0_attn_ref(x, g1, Wq, Wkv, Wout, g2):
        import jax, jax.numpy as jnp
        import numpy as np
        DIM = 128
        HEADS = 16
        DIM_HEAD = 64
        SCALE = 16.0
        EPS = 1e-05

        def layernorm(x, g):
            mean = jnp.mean(x, axis=-1, keepdims=True)
            var = jnp.var(x, axis=-1, keepdims=True)
            return (x - mean) * jax.lax.rsqrt(var + EPS) * g

        def l2norm(t):
            return t / jnp.maximum(jnp.linalg.norm(t, axis=-1, keepdims=True), 1e-12)
        b, n, _ = x.shape
        xn = layernorm(x, g1)
        q = xn @ Wq.T
        kv = xn @ Wkv.T
        k, v = (kv[..., :DIM_HEAD], kv[..., DIM_HEAD:])
        q = q.reshape(b, n, HEADS, DIM_HEAD).transpose(0, 2, 1, 3)
        q = q * SCALE
        q, k = (l2norm(q), l2norm(k))
        srt = np.sqrt(SCALE).astype(np.float32)
        q, k = (q * srt, k * srt)
        sim = jnp.einsum('bhid,bjd->bhij', q, k)
        max_neg = -jnp.finfo(sim.dtype).max
        causal_mask = jnp.triu(jnp.ones((n, n), dtype=bool), 1)
        sim = jnp.where(causal_mask, max_neg, sim)
        attn = jax.nn.softmax(sim.astype(jnp.float32), axis=-1).astype(sim.dtype)
        out = jnp.einsum('bhij,bjd->bhid', attn, v)
        out = out.transpose(0, 2, 1, 3).reshape(b, n, HEADS * DIM_HEAD)
        out = out @ Wout.T
        return layernorm(out, g2)

    def _L0_ffn_ref(x, w_g, c_fc, c_proj):
        import jax, jax.numpy as jnp
        import numpy as np
        import math
        N_EXP = 8
        TOP_K = 2
        CAPACITY_FACTOR = 1.25

        def _capacity(num_tokens):
            cap = math.floor(TOP_K * CAPACITY_FACTOR * num_tokens / N_EXP)
            cap += cap % 2
            return int(cap)
        B, C, d = x.shape
        T = B * C
        cap = _capacity(T)
        xt = x.reshape(T, d)
        logits = xt @ w_g
        top_v, top_i = jax.lax.top_k(logits, TOP_K)
        full = jnp.full_like(logits, -jnp.inf)
        full = full.at[jnp.arange(T)[:, None], top_i].set(top_v)
        probs = jax.nn.softmax(full, axis=-1)
        exp_mask = jax.nn.one_hot(top_i, N_EXP, dtype=jnp.int32)
        exp_mask = jnp.transpose(exp_mask, (1, 0, 2))
        exp_rank = jnp.cumsum(exp_mask.reshape(TOP_K * T, N_EXP), axis=0) - 1
        exp_rank = exp_rank.reshape(TOP_K, T, N_EXP)
        exp_mask = exp_mask * (exp_rank < cap).astype(jnp.int32)
        exp_rank = jnp.sum(exp_mask * exp_rank, axis=-1)
        exp_weights = exp_mask.astype(x.dtype) * probs[None]
        rank_oh = jax.nn.one_hot(exp_rank, cap, dtype=x.dtype)
        cb_weight = jnp.einsum('kte,ktc->tec', exp_weights, rank_oh)
        sec_mask = (cb_weight != 0).astype(x.dtype)
        exp_batches = jnp.einsum('tec,td->ecd', sec_mask, xt)
        h = jax.nn.gelu(jnp.einsum('ecd,edf->ecf', exp_batches, c_fc), approximate=False)
        exp_out = jnp.einsum('ecf,efd->ecd', h, c_proj)
        out = cb_weight.reshape(T, N_EXP * cap) @ exp_out.reshape(N_EXP * cap, d)
        return out.reshape(B, C, d)
    x = L0_attn_x
    x = x + _L0_attn_ref(_layernorm(x, axis=-1), L0_attn_g1, L0_attn_Wq, L0_attn_Wkv, L0_attn_Wout, L0_attn_g2)
    x = x + _L0_ffn_ref(_layernorm(x, axis=-1), L0_ffn_w_g, L0_ffn_c_fc, L0_ffn_c_proj)
    return x

_drawn_inputs = setup_inputs


def setup_inputs(seed=0):
    import zlib

    import numpy as np

    out = dict(_drawn_inputs(seed))
    spreads = {'L0_attn_g1': (1.0, 0.2), 'L0_attn_g2': (1.0, 0.2)}
    factors = {}
    for name, (base, spread) in spreads.items():
        noise = np.random.default_rng([zlib.crc32(name.encode()), seed]).standard_normal(out[name].shape)
        drawn = base * np.exp(spread * noise) if base else spread * noise
        out[name] = jnp.asarray(drawn.astype(out[name].dtype))
    for name, factor in factors.items():
        out[name] = (out[name] * factor).astype(out[name].dtype)
    return out
```

```python
from contextlib import ExitStack

import numpy as np

import concourse.bass as bass
from concourse import mybir

ALU = mybir.AluOpType
ACT = mybir.ActivationFunctionType
F32 = mybir.dt.float32
BF16 = mybir.dt.bfloat16
F32R = mybir.dt.float32r
U32 = mybir.dt.uint32
I32 = mybir.dt.int32
AX_X = mybir.AxisListType.X

P = 128
TOPK = 2
EPS = 1e-5
SCALE = 16.0
CAPACITY_FACTOR = 1.25

A_JOBS = {
    1: [["xnT"], ["kv"], ["q0"]],
    2: [["q1"], ["q2"], ["q3"]],
    3: [["q4"], ["q5"], ["q6"]],
    4: [["q7"], ["qT0"], ["qT1"]],
    5: [["qT2"], ["qT3"], []],
    6: [["qT4"], ["qT5"], []],
    7: [["qT6"], ["kT"], ["qT7"]],
}
Q_SUMS = {2: [0], 3: [1, 2, 3], 4: [4, 5, 6], 5: [7]}
Q_SCALES = {3: 0, 5: 1}
ROOT_STEPS = 10


def build(nc, x, g1, wqT, wkvT, woT, g2, w_g, c_fc, c_proj, out):
    B, N, D = x.shape
    NT = N // P
    T = B * N
    HD = wqT.shape[1]
    DH = wkvT.shape[1] // 2
    H = HD // DH
    PAIRS = H // 2
    E = w_g.shape[1]
    F = c_fc.shape[2]
    FC = F // P
    CAP = int(TOPK * CAPACITY_FACTOR * T / E)
    CAP += CAP % 2
    CT = CAP // P
    GT = 2
    GR = CT // GT
    ROW = D + 2
    FAR = 1.0e6
    TINY_Q = (1e-12 / SCALE) ** 2
    TINY_K = 1e-24
    PADS = 16
    assert D == P and DH == 64 and NT == 4 and PAIRS == 8 and CT % GT == 0 and E % 2 == 0

    x_t = x.rearrange("b (t p) d -> b p t d", p=P)
    out_t = out.rearrange("b (t p) d -> p (b t) d", p=P)
    fc_t = c_fc
    proj_t = c_proj.rearrange("e (c p) d -> e p c d", p=P)

    dispatch = nc.dram_tensor("dispatch", [E * CAP, ROW], F32, kind="Internal").ap()
    combine = nc.dram_tensor("combine", [TOPK * T, D], F32, kind="Internal").ap()
    dispatch_e = dispatch.rearrange("(e t p) r -> e p t r", e=E, p=P)
    dispatch_init = dispatch.rearrange("(p i q) r -> p i (q r)", p=P, q=4)
    combine_init = combine.rearrange("(p i q) r -> p i (q r)", p=P, q=4)
    combine_k = combine.rearrange("(k t p) d -> k p t d", k=TOPK, p=P)

    with ExitStack() as ctx:
        def sb(name, shape, dt=F32):
            return ctx.enter_context(nc.sbuf_tensor(name, shape, dt))

        def ps(name, shape, dt=F32):
            return ctx.enter_context(nc.psum_tensor(name, shape, dt))

        def sem(name):
            return ctx.enter_context(nc.semaphore(name))

        wq_hi = sb("wq_hi", [P, HD], F32R)
        wq_lo = sb("wq_lo", [P, HD], F32R)
        wkv_hi = sb("wkv_hi", [P, 2 * DH], F32R)
        wkv_lo = sb("wkv_lo", [P, 2 * DH], F32R)
        wo_sb = sb("wo_sb", [P, PAIRS, D])
        wg_sb = sb("wg_sb", [P, E])
        g1_col = sb("g1_col", [P, 1])
        g2_row = sb("g2_row", [P, D])
        ident = sb("ident", [P, P])
        before = sb("before", [P, P], BF16)
        ones = sb("ones", [P, P], BF16)
        e_down = sb("e_down", [P, NT, E])
        token_id = sb("token_id", [P, NT])
        zero_rows = sb("zero_rows", [P, 4 * D])
        pad_rows = sb("pad_rows", [P, 4, ROW])
        x_in = sb("x_in", [P, NT, D])
        ln_stats = sb("ln_stats", [P, NT, 6])
        ln_mv = sb("ln_mv", [P, NT, 2])
        ln_var = sb("ln_var", [P, NT])
        ln_tmp = sb("ln_tmp", [P, NT])
        ln_rstd = sb("ln_rstd", [P, NT])
        xn_once = sb("xn_once", [P, NT, D])
        xn = sb("xn", [P, NT, D])
        xnT_hi = sb("xnT_hi", [P, N], F32R)
        xnT_lo = sb("xnT_lo", [P, N], F32R)
        kv_sb = sb("kv_sb", [P, NT, 2 * DH])
        k_sq = sb("k_sq", [P, NT, DH])
        k_ss = sb("k_ss", [P, NT])
        k_tmp = sb("k_tmp", [P, NT])
        k_rn = sb("k_rn", [P, NT])
        k_two = sb("k_two", [P, NT, 2, DH])
        q_tok = sb("q_tok", [P, NT, HD])
        q_sq = sb("q_sq", [P, 8, N])
        q_ss = sb("q_ss", [P, NT, 8])
        q_tmp = sb("q_tmp", [P, NT, 8])
        q_rn = sb("q_rn", [P, NT, 8])
        q_unit = sb("q_unit", [P, 2, NT, 8])
        kT_hi = sb("kT_hi", [P, N], F32R)
        kT_lo = sb("kT_lo", [P, N], F32R)
        qT = sb("qT", [P, PAIRS, 2, N], F32R)
        v_one = sb("v_one", [P, NT, DH + 1])
        probs = sb("probs", [P, 2, 2, 1280])
        rsum = sb("rsum", [P, 2, NT])
        o_tok = sb("o_tok", [P, 2, NT, 2 * DH])
        oT = sb("oT", [P, PAIRS, N])
        x_res = sb("x_res", [P, NT, D])
        y_tok = sb("y_tok", [P, NT, D])
        yn = sb("yn", [P, NT, D])
        x1_all = sb("x1_all", [P, B * NT, D])
        c_stats = sb("c_stats", [P, NT, 6])
        c_mv = sb("c_mv", [P, NT, 2])
        c_var = sb("c_var", [P, NT])
        c_tmp = sb("c_tmp", [P, NT])
        c_rstd = sb("c_rstd", [P, NT])
        rows = sb("rows", [P, NT, TOPK, ROW])
        x1T = sb("x1T", [P, N])
        logits = sb("logits", [P, NT, E])
        lg_rest = sb("lg_rest", [P, NT, E])
        eq = sb("eq", [P, NT, E])
        top = sb("top", [P, TOPK, NT])
        pick = sb("pick", [P, TOPK, NT])
        mask = sb("mask", [P, NT, TOPK, E], BF16)
        gap = sb("gap", [P, NT])
        gap_exp = sb("gap_exp", [P, NT])
        den = sb("den", [P, NT])
        w1 = sb("w1", [P, NT])
        count = sb("count", [P, TOPK, E])
        rank = sb("rank", [P, NT, TOPK, E])
        rank_sel = sb("rank_sel", [P, NT, TOPK])
        first_sel = sb("first_sel", [P, NT, E])
        first_cnt = sb("first_cnt", [P, NT])
        place = sb("place", [P, NT, TOPK])
        over = sb("over", [P, NT, TOPK])
        slot_f = sb("slot_f", [P, NT, TOPK])
        slot_u = sb("slot_u", [P, NT, TOPK], U32)
        fc_sb = [sb(f"fc_sb{u}", [P, F]) for u in range(2)]
        proj_sb = [sb(f"proj_sb{u}", [P, FC, D]) for u in range(2)]
        xt = [sb(f"xt{u}", [P, CT, ROW]) for u in range(2)]
        dest_u = [sb(f"dest_u{u}", [P, CT], U32) for u in range(2)]
        xtT = sb("xtT", [P, 2, GT * P])
        hT = sb("hT", [P, 2, FC, GT * P])
        y_sb = sb("y_sb", [P, 2, GT, D])

        hT_flat = hT[:].rearrange("p a c n -> p (a c n)")
        wq_in_sb = hT_flat[:, 0:HD]
        wkv_in_sb = hT_flat[:, HD:HD + 2 * DH]

        scores = [ps(f"scores{i}", [P, 2, 512]) for i in range(2)]
        pv = [ps(f"pv{i}", [P, 512]) for i in range(2)]
        bank_a = ps("bank_a", [P, 512])
        bank_c = ps("bank_c", [P, 512])
        pv_v = [t[:, 0:NT * (DH + 1)].rearrange("p (t d) -> p t d", t=NT) for t in pv]
        h_ps = [t[:].rearrange("p a (c n) -> p (a c) n", n=GT * P) for t in scores]

        (wq_in, wkv_in, wo_in, wg_in, g_in, init_done, x_loaded, xres_loaded,
         consts_ready, pool_const, memset_ready) = [sem(n) for n in (
            "wq_in", "wkv_in", "wo_in", "wg_in", "g_in", "init_done", "x_loaded", "xres_loaded",
            "consts_ready", "pool_const", "memset_ready")]
        (scores_ready, exp_done, masked, pv_ready, o_normed) = [sem(n) for n in (
            "scores_ready", "exp_done", "masked", "pv_ready", "o_normed")]
        (xn_once_ready, xn_ready, xnT_ps, xnT_hi_ready, xnT_ready, kv_ps, kv_out, q_ps, q_squared,
         q_summed, q_root, q_normed, k_root, k_normed, kT_ps, kT_hi_ready, kT_ready, qT_ps, qT_hi_ready, qT_ready,
         v_ready, w_hi_ready, w_split) = [sem(n) for n in (
            "xn_once_ready", "xn_ready", "xnT_ps", "xnT_hi_ready", "xnT_ready", "kv_ps", "kv_out", "q_ps",
            "q_squared", "q_summed", "q_root", "q_normed", "k_root", "k_normed", "kT_ps", "kT_hi_ready", "kT_ready",
            "qT_ps", "qT_hi_ready", "qT_ready", "v_ready", "w_hi_ready", "w_split")]
        (oT_ps, oT_ready, y_ps, y_copied, y_normed, y_scaled, x1_ready, rows_ready, x1T_ps, x1T_ready, lg_ps,
         lg_ready, gap_ready, gap_exp_ready, mask_ready, rank_ps, rank_out, slots_ready, dispatched) = [sem(n) for n in (
            "oT_ps", "oT_ready", "y_ps", "y_copied", "y_normed", "y_scaled", "x1_ready", "rows_ready", "x1T_ps",
            "x1T_ready", "lg_ps", "lg_ready", "gap_ready", "gap_exp_ready", "mask_ready", "rank_ps", "rank_out",
            "slots_ready", "dispatched")]
        (ln_step, k_step, qn_step, rs_step, c_step, r_step, rank_step) = [sem(n) for n in (
            "ln_step", "k_step", "qn_step", "rs_step", "c_step", "r_step", "rank_step")]
        waits_apart = sem("waits_apart")
        w_loaded = [sem(f"w_loaded{u}") for u in range(2)]
        xt_loaded = [sem(f"xt_loaded{u}") for u in range(2)]
        (xtT_ps, xtT_ready, h_ready, gelu_done, y2_ps, y2_ready, dest_ready) = [sem(n) for n in (
            "xtT_ps", "xtT_ready", "h_ready", "gelu_done", "y2_ps", "y2_ready", "dest_ready")]
        sent = [sem(f"sent{i}") for i in range(2)]
        comb_loaded = [sem(f"comb_loaded{i}") for i in range(4)]
        (comb_sum, out_ready, stored) = [sem(n) for n in ("comb_sum", "out_ready", "stored")]

        block = ctx.enter_context(nc.Block())

        def past(n):
            return max(n, 0) if isinstance(n, int) else n

        def batches(eng, run):
            run(0, False, True)
            with eng.Fori(1, B - 1) as b:
                run(b, True, True)
            run(B - 1, True, False)

        def score_blocks(s):
            return {0: [(0, 0, 512, 0)], 1: [(1, 128, 384, 0), (3, 384, 128, 384)], 2: [(2, 256, 256, 0)]}[s]

        def prob_block(jt, it):
            return {0: it * P, 1: 512 + (it - 1) * P, 2: 1024 + (it - 2) * P, 3: 896}[jt]

        W_ITERS = E // 2
        GROUPS = 2 * GR

        def expert_pairs(eng, run):
            run(0)
            with eng.Fori(1, W_ITERS - 1) as m:
                run(m)
            run(W_ITERS - 1)

        comb_a = q_sq[:].rearrange("p a n -> p (a n)").rearrange("p (t d) -> p t d", d=D)
        comb_b = oT[:].rearrange("p a n -> p (a n)").rearrange("p (t d) -> p t d", d=D)

        @block.sync
        def _(sp):
            sp.dma_start(x_in[:], x_t[0]).then_inc(x_loaded, 16)
            sp.dma_start(wkv_in_sb, wkvT).then_inc(wkv_in, 16)
            sp.dma_start(wq_in_sb, wqT).then_inc(wq_in, 16)
            sp.dma_start(x_res[:], x_t[0]).then_inc(xres_loaded, 16)
            sp.dma_start(wo_sb[:], woT.rearrange("(c p) d -> p c d", p=P)).then_inc(wo_in, 16)
            sp.dma_start(wg_sb[:], w_g).then_inc(wg_in, 16)
            sp.wait_ge(memset_ready, 3)
            sp.dma_start(combine_init, zero_rows[:].unsqueeze(1).broadcast_to(
                [P, combine_init.shape[1], 4 * D])).then_inc(init_done, 16)

            def next_x(b):
                sp.wait_ge(xn_ready, past(b))
                sp.dma_start(x_in[:], x_t[b]).then_inc(x_loaded, 16)

            next_x(1)
            with sp.Fori(2, B) as b:
                next_x(b)
                sp.wait_ge(x1_ready, past(b - 1))
                sp.dma_start(x_res[:], x_t[b - 1]).then_inc(xres_loaded, 16)
            sp.wait_ge(x1_ready, past(B - 1))
            sp.dma_start(x_res[:], x_t[B - 1]).then_inc(xres_loaded, 16)

            def expert_loads(m, first):
                for u in range(2):
                    e = m * 2 + u
                    if not first:
                        sp.wait_ge(y2_ps, past(GROUPS * (m - 1) + GR * (u + 1)))
                    sp.dma_start(fc_sb[u][:], fc_t[e]).then_inc(w_loaded[u], 16)
                    sp.dma_start(proj_sb[u][:], proj_t[e]).then_inc(w_loaded[u], 16)
                    if first and u == 0:
                        sp.wait_ge(dispatched, PADS + 128 * B)
                    if not first:
                        sp.wait_ge(y2_ready, past(GROUPS * (m - 1) + GR * (u + 1)))
                    sp.dma_start(xt[u][:], dispatch_e[e]).then_inc(xt_loaded[u], 16)

            expert_loads(0, True)
            with sp.Fori(1, W_ITERS) as m:
                expert_loads(m, False)

            for i in range(2):
                sp.wait_ge(sent[i], 16 * GT * W_ITERS * GR)
            for c in range(4):
                t0 = c * 8
                sp.dma_start(comb_a[:, t0:t0 + 8, :], combine_k[0][:, t0:t0 + 8, :]).then_inc(comb_loaded[c], 16)
                sp.dma_start(comb_b[:, t0:t0 + 8, :], combine_k[1][:, t0:t0 + 8, :]).then_inc(comb_loaded[c], 16)
            for c in range(4):
                t0 = c * 8
                sp.wait_ge(out_ready, c + 1)
                sp.dma_start(out_t[:, t0:t0 + 8, :], x1_all[:, t0:t0 + 8, :]).then_inc(stored, 16)
            sp.wait_ge(stored, 64)

        @block.gpsimd
        def _(pool):
            nc.gpsimd.dma_start(g1_col[:], g1.rearrange("(p o) -> p o", o=1)).then_inc(g_in, 16)
            nc.gpsimd.dma_start(g2_row[:], g2.rearrange("(o d) -> o d", o=1).broadcast_to([P, D])).then_inc(g_in, 16)
            nc.gpsimd.memset(ident[:], 0.0).then_inc(pool_const, 1)
            nc.gpsimd.memset(before[:], 1.0).then_inc(pool_const, 1)
            nc.gpsimd.memset(ones[:], 1.0).then_inc(pool_const, 1)
            nc.gpsimd.iota(e_down[:], pattern=[[0, NT], [-1, E]], base=E, channel_multiplier=0,
                           allow_small_or_imprecise_dtypes=True).then_inc(pool_const, 1)
            nc.gpsimd.iota(token_id[:], pattern=[[P, NT]], base=0, channel_multiplier=1,
                           allow_small_or_imprecise_dtypes=True).then_inc(pool_const, 1)
            pool.wait_ge(pool_const, 5)
            nc.gpsimd.affine_select(out=ident[:], in_=ident[:], compare_op=ALU.not_equal, fill=1.0, base=0,
                                    pattern=[[-1, P]], channel_multiplier=1).then_inc(consts_ready, 1)
            nc.gpsimd.affine_select(out=before[:], in_=before[:], compare_op=ALU.is_gt, fill=0.0, base=0,
                                    pattern=[[1, P]], channel_multiplier=-1).then_inc(consts_ready, 1)

            def q_scale(n, half, its):
                pool.wait_ge(q_root, 2 * n + half + 1)
                for it in its:
                    q = q_tok[:, it, half * 512:half * 512 + 512].rearrange("p (h d) -> p h d", d=DH)
                    nc.gpsimd.tensor_tensor(q, q, q_unit[:, half, it, :].unsqueeze(2).broadcast_to([P, 8, DH]),
                                            ALU.mult).then_inc(q_normed, 1)

            def causal(b, p, s):
                pool.wait_ge(exp_done, 24 * b + 3 * p + s + 1)
                pool.sem_inc(waits_apart, 1)
                for jt, i0, n, c in score_blocks(s):
                    v = probs[:, p % 2, :, 512 * s + c:512 * s + c + P]
                    last = nc.gpsimd.affine_select(out=v, in_=v, compare_op=ALU.is_ge, fill=0.0, base=0,
                                                   pattern=[[0, 2], [1, P]], channel_multiplier=-1)
                last.then_inc(masked, 1)

            def dispatch_rows(b):
                pool.wait_ge(slots_ready, b + 1)
                pool.wait_ge(dispatched, PADS + 128 * b)
                pool.sem_inc(waits_apart, 1)
                for k in (1, 0):
                    for it in range(NT):
                        pool.indirect_dma_start(
                            out=dispatch, out_offset=bass.IndirectOffsetOnAxis(ap=slot_u[:, it, k:k + 1], axis=0),
                            in_=rows[:, it, k, :], in_offset=None, bounds_check=E * CAP - 1,
                            oob_is_err=False).then_inc(dispatched, 16)

            pool.wait_ge(memset_ready, 4)
            pool.dma_start(dispatch_init, pad_rows[:].rearrange("p q r -> p (q r)").unsqueeze(1).broadcast_to(
                [P, dispatch_init.shape[1], 4 * ROW])).then_inc(dispatched, 16)
            for half in range(2):
                q_scale(0, half, range(NT))

            def run(b, has_prev, has_next):
                for p in range(PAIRS):
                    for s in range(3):
                        causal(b, p, s)
                        if has_next and p in Q_SCALES and s < 2:
                            q_scale(b + 1, Q_SCALES[p], range(2 * s, 2 * s + 2))
                    if p == 7 and has_prev:
                        dispatch_rows(b - 1)

            batches(pool, run)
            dispatch_rows(B - 1)

            pool.wait_ge(init_done, 16)

            def groups(m):
                for u in range(2):
                    pool.wait_ge(dest_ready, 2 * m + u + 1)
                    pool.sem_inc(waits_apart, 1)
                    for r in range(GR):
                        k = GR * u + r
                        pool.wait_ge(y2_ready, GROUPS * m + k + 1)
                        pool.sem_inc(waits_apart, 1)
                        for i in range(GT):
                            t = GT * r + i
                            pool.indirect_dma_start(
                                out=combine, out_offset=bass.IndirectOffsetOnAxis(ap=dest_u[u][:, t:t + 1], axis=0),
                                in_=y_sb[:, k % 2, i, :], in_offset=None, bounds_check=TOPK * T - 1,
                                oob_is_err=False).then_inc(sent[k % 2], 16)

            expert_pairs(pool, groups)
            for i in range(2):
                pool.wait_ge(sent[i], 16 * GT * W_ITERS * GR)

        @block.scalar
        def _(act):
            def q_copy(n, j):
                half, it = divmod(j, NT)
                act.wait_ge(q_ps, 8 * n + j + 1)
                act.wait_ge(qT_ps, past(8 * n))
                act.wait_ge(q_summed, past(8 * n))
                nc.scalar.copy(q_tok[:, it, half * 512:half * 512 + 512], bank_a[:])
                nc.scalar.activation(q_sq[:, j, :], bank_a[:], ACT.Square).then_inc(q_squared, 1)

            def qT_copy(n, p):
                act.wait_ge(qT_ps, 8 * n + p + 1)
                nc.scalar.copy(qT[0:DH, p, 0, :], bank_a[0:DH, :])
                nc.scalar.copy(qT[DH:P, p, 1, :], bank_a[DH:P, :]).then_inc(qT_hi_ready, 1)

            def oT_copy(b, p):
                act.wait_ge(oT_ps, 8 * b + p + 1)
                if p == 0:
                    act.wait_ge(y_ps, past(NT * b))
                nc.scalar.copy(oT[:, p, :], bank_c[:]).then_inc(oT_ready, 1)

            def jobs(n, p, place):
                for job in A_JOBS[p][place] if p in A_JOBS else []:
                    if job.startswith("qT"):
                        qT_copy(n, int(job[2:]))
                    elif job.startswith("q"):
                        q_copy(n, int(job[1:]))

            def exp(b, p, s):
                act.wait_ge(scores_ready, 24 * b + 3 * p + s + 1)
                act.wait_ge(pv_ready, past(16 * b + 2 * (p - 1)))
                n = (512, 512, 256)[s]
                c = 512 * s
                slot = (p + s) % 2
                nc.scalar.activation(probs[:, p % 2, :, c:c + n], scores[slot][:, :, 0:n], ACT.Exp,
                                     scale=SCALE).then_inc(exp_done, 1)

            def gap_exponential(b):
                act.wait_ge(gap_ready, b + 1)
                nc.scalar.activation(gap_exp[:], gap[:], ACT.Exp).then_inc(gap_exp_ready, 1)

            for j in range(8):
                q_copy(0, j)
            for p in range(PAIRS):
                qT_copy(0, p)

            def run(b, has_prev, has_next):
                for p in range(PAIRS):
                    exp(b, p, 0)
                    exp(b, p, 1)
                    if p < 2 and has_prev:
                        oT_copy(b - 1, p + 6)
                    if p >= 3:
                        oT_copy(b, 0 if p == 3 else p - 2)
                    if has_next:
                        jobs(b + 1, p, 0)
                    exp(b, p, 2)
                    if has_next:
                        jobs(b + 1, p, 1)
                    if p == 3:
                        oT_copy(b, 1)
                    if has_next:
                        jobs(b + 1, p, 2)
                    if p == 6 and has_prev:
                        gap_exponential(b - 1)

            batches(act, run)
            oT_copy(B - 1, 6)
            oT_copy(B - 1, 7)
            gap_exponential(B - 1)

            def groups(m):
                for k in range(GROUPS):
                    g = GROUPS * m + k
                    act.wait_ge(h_ready, g + 1)
                    act.wait_ge(y2_ps, past(g - 1))
                    nc.scalar.activation(hT[:, k % 2], h_ps[k % 2], ACT.Gelu).then_inc(gelu_done, 1)

            expert_pairs(act, groups)

        @block.tensor
        def _(pe):
            def scores_step(b, p, s):
                g = 24 * b + 3 * p + s
                pe.wait_ge(exp_done, past(g - 1))
                if s == 0:
                    pe.wait_ge(qT_ready, 8 * b + p + 1)
                    if p == 0:
                        pe.wait_ge(kT_ready, b + 1)
                slot = scores[(p + s) % 2]
                for jt, i0, n, c in score_blocks(s):
                    for k_part in (kT_hi, kT_lo):
                        for head in range(2):
                            last = nc.tensor.matmul(slot[:, head, c:c + n], k_part[:, jt * P:jt * P + P],
                                                    qT[:, p, head, i0:i0 + n], start=(k_part is kT_hi),
                                                    stop=(k_part is kT_lo))
                last.then_inc(scores_ready, 1)

            def values(b, p, head):
                h = 16 * b + 2 * p + head
                pe.wait_ge(o_normed, past(h - 1))
                pe.wait_ge(masked, 24 * b + 3 * p + 3)
                if p == 0:
                    pe.wait_ge(v_ready, b + 1)
                for it in range(NT):
                    for jt in range(it + 1):
                        c = prob_block(jt, it)
                        last = nc.tensor.matmul(pv_v[head][:, it, :], probs[:, p % 2, head, c:c + P],
                                                v_one[:, jt, :], start=(jt == 0), stop=(jt == it))
                last.then_inc(pv_ready, 1)

            def a_job(n, job):
                if job == "xnT":
                    pe.wait_ge(xn_ready, n + 1)
                    pe.wait_ge(qT_ready, past(8 * n))
                    for it in range(NT):
                        last = nc.tensor.transpose(bank_a[:, it * P:it * P + P], xn[:, it, :], ident[:])
                    last.then_inc(xnT_ps, 1)
                elif job == "kv":
                    pe.wait_ge(xnT_ready, n + 1)
                    for it in range(NT):
                        tile = slice(it * P, it * P + P)
                        nc.tensor.matmul(bank_a[:, tile], xnT_hi[:, tile], wkv_hi[:], start=True, stop=False)
                        nc.tensor.matmul(bank_a[:, tile], xnT_hi[:, tile], wkv_lo[:], start=False, stop=False)
                        last = nc.tensor.matmul(bank_a[:, tile], xnT_lo[:, tile], wkv_hi[:], start=False, stop=True)
                    last.then_inc(kv_ps, 1)
                elif job == "kT":
                    pe.wait_ge(k_normed, n + 1)
                    pe.wait_ge(qT_ready, 8 * n + 7)
                    for it in range(NT):
                        last = nc.tensor.transpose(bank_a[:, it * P:it * P + P],
                                                   k_two[:, it].rearrange("p a d -> p (a d)"), ident[:])
                    last.then_inc(kT_ps, 1)
                elif job.startswith("qT"):
                    p = int(job[2:])
                    pe.wait_ge(q_normed, 8 * n + (4 if p < 4 else 8))
                    if p == 0:
                        pe.wait_ge(q_squared, 8 * n + 8)
                    elif p == 7:
                        pe.wait_ge(kT_ready, n + 1)
                    else:
                        pe.wait_ge(qT_ready, 8 * n + p)
                    for it in range(NT):
                        last = nc.tensor.transpose(bank_a[:, it * P:it * P + P],
                                                   q_tok[:, it, p * P:p * P + P], ident[:])
                    last.then_inc(qT_ps, 1)
                else:
                    j = int(job[1:])
                    half, it = divmod(j, NT)
                    if j == 0:
                        pe.wait_ge(kv_out, n + 1)
                    else:
                        pe.wait_ge(q_squared, 8 * n + j)
                    tile, heads = slice(it * P, it * P + P), slice(half * 512, half * 512 + 512)
                    nc.tensor.matmul(bank_a[:], xnT_hi[:, tile], wq_hi[:, heads], start=True, stop=False)
                    nc.tensor.matmul(bank_a[:], xnT_hi[:, tile], wq_lo[:, heads], start=False, stop=False)
                    nc.tensor.matmul(bank_a[:], xnT_lo[:, tile], wq_hi[:, heads],
                                     start=False, stop=True).then_inc(q_ps, 1)

            def o_transposes(b, p, after=None):
                pe.wait_ge(o_normed, 16 * b + 2 * p + 2)
                pe.wait_ge(oT_ready, 8 * b + p)
                if after is not None:
                    pe.wait_ge(*after)
                for it in range(NT):
                    last = nc.tensor.transpose(bank_c[:, it * P:it * P + P], o_tok[:, p % 2, it, :], ident[:])
                last.then_inc(oT_ps, 1)

            def out_projection(b, it):
                pe.wait_ge(oT_ready, 8 * b + 8)
                if it > 0:
                    pe.wait_ge(y_copied, NT * b + it)
                for c in range(PAIRS):
                    last = nc.tensor.matmul(bank_c[:, 0:D], oT[:, c, it * P:it * P + P],
                                            wo_sb[:, c, :], start=(c == 0), stop=(c == PAIRS - 1))
                last.then_inc(y_ps, 1)

            def x1_transposes(b, last_batch):
                pe.wait_ge(rows_ready, b + 1)
                if not last_batch:
                    pe.wait_ge(oT_ready, 8 * (b + 1) + 4)
                for it in range(NT):
                    last = nc.tensor.transpose(bank_c[:, it * P:it * P + P], rows[:, it, 0, 0:D], ident[:])
                last.then_inc(x1T_ps, 1)

            def router(b, last_batch):
                pe.wait_ge(x1T_ready, b + 1)
                if not last_batch:
                    pe.wait_ge(oT_ready, 8 * (b + 1) + 5)
                for it in range(NT):
                    last = nc.tensor.matmul(bank_c[:, it * E:it * E + E], x1T[:, it * P:it * P + P],
                                            wg_sb[:], start=True, stop=True)
                last.then_inc(lg_ps, 1)

            def ranks(b, last_batch):
                pe.wait_ge(mask_ready, b + 1)
                if not last_batch:
                    pe.wait_ge(oT_ready, 8 * (b + 1) + 6)
                W2 = TOPK * E
                m = mask[:].rearrange("p t k e -> p t (k e)")
                for it in range(NT + 1):
                    for jt in range(min(it + 1, NT)):
                        last = nc.tensor.matmul(bank_c[:, it * W2:it * W2 + W2],
                                                before[:] if jt == it else ones[:], m[:, jt, :],
                                                start=(jt == 0), stop=(jt == min(it, NT - 1)))
                last.then_inc(rank_ps, 1)

            pe.wait_ge(consts_ready, 2)
            pe.wait_ge(w_split, 2)
            for job in ["xnT", "kv"] + [f"q{j}" for j in range(8)] + [f"qT{p}" for p in range(7)] + ["kT", "qT7"]:
                a_job(0, job)
            pe.wait_ge(wo_in, 16)
            pe.wait_ge(wg_in, 16)

            def run(b, has_prev, has_next):
                for p in range(PAIRS):
                    pb, pp = (b, p - 1) if p >= 1 else (b - 1, 7)
                    has_values = p >= 1 or has_prev

                    def jobs(place):
                        if has_next and p in A_JOBS:
                            for job in A_JOBS[p][place]:
                                a_job(b + 1, job)

                    scores_step(b, p, 0)
                    if p < 2 and has_prev:
                        o_transposes(b - 1, p + 6, (rank_out, b) if p == 0 else None)
                    if p == 2 and has_prev:
                        out_projection(b - 1, 0)
                    if p >= 3:
                        o_pair = 0 if p == 3 else p - 2
                        after = {3: (y_copied, NT * b), 6: (x1T_ready, b), 7: (lg_ready, b)}.get(p)
                        o_transposes(b, o_pair, after if has_prev else None)
                    scores_step(b, p, 1)
                    if has_values:
                        values(pb, pp, 0)
                    jobs(0)
                    if p == 2 and has_prev:
                        out_projection(b - 1, 1)
                    scores_step(b, p, 2)
                    if has_prev and p == 5:
                        x1_transposes(b - 1, False)
                    if has_prev and p == 6:
                        router(b - 1, False)
                    if has_prev and p == 7:
                        ranks(b - 1, False)
                    jobs(1)
                    if p == 2 and has_prev:
                        out_projection(b - 1, 2)
                    if has_values:
                        values(pb, pp, 1)
                    if p == 2 and has_prev:
                        out_projection(b - 1, 3)
                    if p == 3:
                        o_transposes(b, 1)
                    jobs(2)

            batches(pe, run)
            b = B - 1
            o_transposes(b, 6, (rank_out, b + 1))
            values(b, 7, 0)
            values(b, 7, 1)
            o_transposes(b, 7)
            for it in range(NT):
                out_projection(b, it)
            x1_transposes(b, True)
            router(b, True)
            ranks(b, True)

            banks = [bank_a, bank_c]

            def transposes(m, k):
                u, r = divmod(k, GR)
                if r == 0:
                    pe.wait_ge(xt_loaded[u], 16 * (m + 1))
                pe.wait_ge(xtT_ready, past(GROUPS * m + k - 1))
                for i in range(GT):
                    last = nc.tensor.transpose(banks[k % 2][:, i * P:i * P + P], xt[u][:, GT * r + i, 0:D], ident[:])
                last.then_inc(xtT_ps, 1)

            def up(m, k):
                u, r = divmod(k, GR)
                g = GROUPS * m + k
                if r == 0:
                    pe.wait_ge(w_loaded[u], 32 * (m + 1))
                pe.wait_ge(xtT_ready, g + 1)
                pe.wait_ge(gelu_done, past(g - 1))
                for c in range(FC):
                    last = nc.tensor.matmul(h_ps[k % 2][:, c, :], fc_sb[u][:, c * P:c * P + P], xtT[:, k % 2, :],
                                            start=True, stop=True)
                last.then_inc(h_ready, 1)

            def down(m, k):
                u = k // GR
                g = GROUPS * m + k
                pe.wait_ge(gelu_done, g + 1)
                pe.wait_ge(y2_ready, past(g - 1))
                for i in range(GT):
                    for c in range(FC):
                        last = nc.tensor.matmul(pv[k % 2][:, i * P:i * P + P], hT[:, k % 2, c, i * P:i * P + P],
                                                proj_sb[u][:, c, :], start=(c == 0), stop=(c == FC - 1))
                last.then_inc(y2_ps, 1)

            pe.wait_ge(rank_out, B + 1)
            transposes(0, 0)

            def groups(m):
                first = isinstance(m, int) and m == 0
                final = isinstance(m, int) and m == W_ITERS - 1
                for k in range(GROUPS):
                    up(m, k)
                    if k < GROUPS - 1:
                        transposes(m, k + 1)
                    elif not final:
                        transposes(m + 1, 0)
                    if k > 0:
                        down(m, k - 1)
                    elif not first:
                        down(m - 1, GROUPS - 1)
                if final:
                    down(m, GROUPS - 1)

            expert_pairs(pe, groups)

        @block.vector
        def _(dve):
            v = nc.vector

            def inverse_root(x, y, t, step, at):
                v.tensor_scalar(y.bitcast(I32), x.bitcast(I32), -0.5, 1597463007.0, ALU.mult, ALU.add).then_inc(step, 1)
                for i in range(3):
                    dve.wait_ge(step, at + 3 * i + 1)
                    v.tensor_tensor(t, x, y, ALU.mult).then_inc(step, 1)
                    dve.wait_ge(step, at + 3 * i + 2)
                    v.scalar_tensor_tensor(out=t, in0=t, scalar=-0.5, in1=y, op0=ALU.mult, op1=ALU.mult).then_inc(step, 1)
                    dve.wait_ge(step, at + 3 * i + 3)
                    v.scalar_tensor_tensor(out=y, in0=t, scalar=1.5, in1=y, op0=ALU.add, op1=ALU.mult).then_inc(step, 1)
                dve.wait_ge(step, at + ROOT_STEPS)

            MOMENT_STEPS = 3 + ROOT_STEPS

            def moments(src, stats, mv, var, rstd, tmp, step, at):
                for it in range(NT):
                    last = v.bn_stats(stats[:, it, :], src[:, it, :])
                last.then_inc(step, 1)
                dve.wait_ge(step, at + 1)
                dve.sem_inc(waits_apart, 1)
                for it in range(NT):
                    last = v.bn_aggr(mv[:, it, :], stats[:, it, :])
                last.then_inc(step, 1)
                dve.wait_ge(step, at + 2)
                v.tensor_scalar(var[:], mv[:, :, 1], EPS, None, ALU.add).then_inc(step, 1)
                dve.wait_ge(step, at + 3)
                inverse_root(var[:], rstd[:], tmp[:], step, at + 3)

            def normalise(src, dst, mv, rstd, done):
                for it in range(NT):
                    last = v.tensor_scalar(dst(it), src[:, it, :], mv[:, it, 0:1], rstd[:, it:it + 1],
                                           ALU.subtract, ALU.mult)
                last.then_inc(done, 1)

            def input_norms(n):
                dve.wait_ge(x_loaded, 16 * (n + 1))
                dve.wait_ge(xnT_ps, past(n))
                moments(x_in, ln_stats, ln_mv, ln_var, ln_rstd, ln_tmp, ln_step, 2 * MOMENT_STEPS * n)
                normalise(x_in, lambda it: xn_once[:, it, :], ln_mv, ln_rstd, xn_once_ready)
                dve.wait_ge(xn_once_ready, n + 1)
                moments(xn_once, ln_stats, ln_mv, ln_var, ln_rstd, ln_tmp, ln_step, 2 * MOMENT_STEPS * n + MOMENT_STEPS)
                normalise(xn_once, lambda it: xn[:, it, :], ln_mv, ln_rstd, xn_ready)

            K_STEPS = 3 + ROOT_STEPS

            def a_job(n, job):
                if job == "xnT":
                    dve.wait_ge(xnT_ps, n + 1)
                    dve.wait_ge(q_ps, past(8 * n))
                    v.tensor_scalar(xnT_hi[:], bank_a[:], g1_col[:, 0:1], None, ALU.mult).then_inc(xnT_hi_ready, 1)
                    dve.wait_ge(xnT_hi_ready, n + 1)
                    v.scalar_tensor_tensor(out=xnT_lo[:], in0=bank_a[:], scalar=g1_col[:, 0:1],
                                           in1=xnT_hi[:].bitcast(F32), op0=ALU.mult,
                                           op1=ALU.subtract).then_inc(xnT_ready, 1)
                elif job == "kv":
                    dve.wait_ge(kv_ps, n + 1)
                    dve.wait_ge(kT_ps, past(n))
                    v.tensor_copy(kv_sb[:].rearrange("p t d -> p (t d)"), bank_a[:]).then_inc(kv_out, 1)
                    dve.wait_ge(kv_out, n + 1)
                    v.tensor_tensor(k_sq[:], kv_sb[:, :, 0:DH], kv_sb[:, :, 0:DH], ALU.mult).then_inc(k_step, 1)
                    dve.wait_ge(k_step, K_STEPS * n + 1)
                    v.tensor_reduce(k_ss[:], k_sq[:], AX_X, ALU.add).then_inc(k_step, 1)
                    dve.wait_ge(k_step, K_STEPS * n + 2)
                    v.tensor_scalar(k_ss[:], k_ss[:], TINY_K, None, ALU.max).then_inc(k_step, 1)
                    dve.wait_ge(k_step, K_STEPS * n + 3)
                    inverse_root(k_ss[:], k_rn[:], k_tmp[:], k_step, K_STEPS * n + 3)
                    for a in range(2):
                        last = v.tensor_tensor(k_two[:, :, a, :], kv_sb[:, :, 0:DH],
                                               k_rn[:].unsqueeze(2).broadcast_to([P, NT, DH]), ALU.mult)
                    last.then_inc(k_normed, 1)
                elif job == "kT":
                    dve.wait_ge(kT_ps, n + 1)
                    dve.wait_ge(scores_ready, past(24 * n))
                    v.tensor_copy(kT_hi[:], bank_a[:]).then_inc(kT_hi_ready, 1)
                    dve.wait_ge(kT_hi_ready, n + 1)
                    v.tensor_tensor(kT_lo[:], bank_a[:], kT_hi[:].bitcast(F32), ALU.subtract).then_inc(kT_ready, 1)
                elif job.startswith("qT"):
                    p = int(job[2:])
                    dve.wait_ge(qT_hi_ready, 8 * n + p + 1)
                    v.tensor_tensor(qT[DH:P, p, 0, :], bank_a[0:DH, :], qT[0:DH, p, 0, :].bitcast(F32), ALU.subtract)
                    v.tensor_tensor(qT[0:DH, p, 1, :], bank_a[DH:P, :], qT[DH:P, p, 1, :].bitcast(F32),
                                    ALU.subtract).then_inc(qT_ready, 1)

            Q_STEPS = 1 + ROOT_STEPS

            def q_sums(n, js):
                for j in js:
                    dve.wait_ge(q_squared, 8 * n + j + 1)
                    v.tensor_reduce(q_ss[:, j % NT, :], q_sq[:, j, :].rearrange("p (h d) -> p h d", d=DH),
                                    AX_X, ALU.add).then_inc(q_summed, 1)
                if js and js[-1] % NT == NT - 1:
                    half = js[-1] // NT
                    at = Q_STEPS * (2 * n + half)
                    dve.wait_ge(q_summed, 8 * n + NT * (half + 1))
                    v.tensor_scalar(q_ss[:], q_ss[:], TINY_Q, None, ALU.max).then_inc(qn_step, 1)
                    dve.wait_ge(qn_step, at + 1)
                    flat = [a[:].rearrange("p t h -> p (t h)") for a in (q_ss, q_rn, q_tmp)]
                    inverse_root(*flat, qn_step, at + 1)
                    dve.wait_ge(q_normed, past(8 * n - 4 + NT * half))
                    v.tensor_copy(q_unit[:, half], q_rn[:]).then_inc(q_root, 1)

            def values_in(b):
                dve.wait_ge(pv_ready, past(16 * b))
                v.tensor_copy(v_one[:, :, 0:DH], kv_sb[:, :, DH:2 * DH]).then_inc(v_ready, 1)

            def o_norm(b, p, head):
                h = 16 * b + 2 * p + head
                dve.wait_ge(pv_ready, h + 1)
                dve.wait_ge(oT_ps, past(8 * b + p - 1))
                v.reciprocal(rsum[:, head, :].unsqueeze(2), pv_v[head][:, :, DH:DH + 1]).then_inc(rs_step, 1)
                dve.wait_ge(rs_step, h + 1)
                v.tensor_tensor(o_tok[:, p % 2, :, head * DH:head * DH + DH], pv_v[head][:, :, 0:DH],
                                rsum[:, head, :].unsqueeze(2).broadcast_to([P, NT, DH]), ALU.mult).then_inc(o_normed, 1)

            def y_copy(b, it):
                dve.wait_ge(y_ps, NT * b + it + 1)
                v.tensor_copy(y_tok[:, it, :], bank_c[:, 0:D]).then_inc(y_copied, 1)

            C_STEPS = 2 * MOMENT_STEPS

            def y_moments(b):
                dve.wait_ge(y_copied, NT * b + NT)
                moments(y_tok, c_stats, c_mv, c_var, c_rstd, c_tmp, c_step, C_STEPS * b)

            def x1_from_y(b):
                dve.wait_ge(xres_loaded, 16 * (b + 1))
                normalise(y_tok, lambda it: yn[:, it, :], c_mv, c_rstd, y_normed)
                dve.wait_ge(y_normed, b + 1)
                v.tensor_tensor(yn[:], yn[:], g2_row[:].unsqueeze(1).broadcast_to([P, NT, D]),
                                ALU.mult).then_inc(y_scaled, 1)
                dve.wait_ge(y_scaled, b + 1)
                v.tensor_tensor(yn[:], yn[:], x_res[:], ALU.add).then_inc(x1_ready, 1)
                dve.wait_ge(x1_ready, b + 1)
                moments(yn, c_stats, c_mv, c_var, c_rstd, c_tmp, c_step, C_STEPS * b + MOMENT_STEPS)

            def x1_norms(b):
                dve.wait_ge(dispatched, PADS + 128 * b)
                normalise(yn, lambda it: rows[:, it, 0, 0:D], c_mv, c_rstd, rows_ready)
                v.tensor_copy(x1_all[:, bass.ds(b * NT, NT), :], yn[:])
                dve.wait_ge(rows_ready, b + 1)
                v.tensor_copy(rows[:, :, 1, 0:D], rows[:, :, 0, 0:D])

            def x1T_copy(b):
                dve.wait_ge(x1T_ps, b + 1)
                v.tensor_copy(x1T[:], bank_c[:]).then_inc(x1T_ready, 1)

            def choose(b):
                dve.wait_ge(lg_ps, b + 1)
                at = 12 * b
                v.tensor_copy(logits[:].rearrange("p t e -> p (t e)"), bank_c[:, 0:NT * E]).then_inc(lg_ready, 1)
                dve.wait_ge(lg_ready, b + 1)
                for k in range(TOPK):
                    src = logits if k == 0 else lg_rest
                    v.tensor_reduce(top[:, k, :], src[:], AX_X, ALU.max).then_inc(r_step, 1)
                    dve.wait_ge(r_step, at + 6 * k + 1)
                    v.tensor_tensor(eq[:], src[:], top[:, k, :].unsqueeze(2).broadcast_to([P, NT, E]),
                                    ALU.is_equal).then_inc(r_step, 1)
                    dve.wait_ge(r_step, at + 6 * k + 2)
                    v.tensor_tensor(eq[:], eq[:], e_down[:], ALU.mult).then_inc(r_step, 1)
                    dve.wait_ge(r_step, at + 6 * k + 3)
                    v.tensor_reduce(pick[:, k, :], eq[:], AX_X, ALU.max).then_inc(r_step, 1)
                    dve.wait_ge(r_step, at + 6 * k + 4)
                    last = v.tensor_tensor(mask[:, :, k, :], e_down[:],
                                           pick[:, k, :].unsqueeze(2).broadcast_to([P, NT, E]), ALU.is_equal)
                    if k == 0:
                        last.then_inc(r_step, 1)
                        dve.wait_ge(r_step, at + 5)
                        v.scalar_tensor_tensor(out=lg_rest[:], in0=mask[:, :, 0, :], scalar=-3.0e38,
                                               in1=logits[:], op0=ALU.mult, op1=ALU.add).then_inc(r_step, 1)
                        dve.wait_ge(r_step, at + 6)
                last.then_inc(mask_ready, 1)
                v.tensor_tensor(gap[:], top[:, 1, :], top[:, 0, :], ALU.subtract).then_inc(gap_ready, 1)
                dve.wait_ge(gap_exp_ready, b + 1)
                v.tensor_scalar(den[:], gap_exp[:], 1.0, None, ALU.add).then_inc(r_step, 1)
                dve.wait_ge(r_step, at + 11)
                v.reciprocal(w1[:], den[:]).then_inc(r_step, 1)
                dve.wait_ge(r_step, at + 12)
                v.tensor_tensor(rows[:, :, 1, D], gap_exp[:], w1[:], ALU.mult)
                v.tensor_copy(rows[:, :, 0, D], w1[:])

            def slots(b):
                dve.wait_ge(rank_ps, b + 1)
                at = 8 * b
                W2 = TOPK * E
                v.tensor_tensor(rank[:].rearrange("p t k e -> p t (k e)"),
                                bank_c[:, 0:NT * W2].rearrange("p (t w) -> p t w", t=NT),
                                count[:].rearrange("p k e -> p (k e)").unsqueeze(1).broadcast_to([P, NT, W2]), ALU.add)
                v.tensor_scalar(rows[:, :, 0, D + 1], token_id[:], 0.0, None, ALU.add)
                v.tensor_scalar(rows[:, :, 1, D + 1], token_id[:], float(T), None, ALU.add).then_inc(rank_step, 1)
                dve.wait_ge(rank_step, at + 1)
                v.tensor_tensor(count[:].rearrange("p k e -> p (k e)"), count[:].rearrange("p k e -> p (k e)"),
                                bank_c[:, NT * W2:NT * W2 + W2], ALU.add).then_inc(rank_out, 1)
                v.tensor_scalar(token_id[:], token_id[:], float(N), None, ALU.add)
                v.tensor_tensor(rank[:].rearrange("p t k e -> p t (k e)"), rank[:].rearrange("p t k e -> p t (k e)"),
                                mask[:].rearrange("p t k e -> p t (k e)"), ALU.mult).then_inc(rank_step, 1)
                dve.wait_ge(rank_step, at + 2)
                dve.wait_ge(rank_out, b + 2)
                v.tensor_tensor(first_sel[:], mask[:, :, 1, :],
                                count[:, 0, :].unsqueeze(1).broadcast_to([P, NT, E]), ALU.mult).then_inc(rank_step, 1)
                dve.wait_ge(rank_step, at + 3)
                v.tensor_reduce(rank_sel[:].rearrange("p t k -> p (t k)"), rank[:].rearrange("p t k e -> p (t k) e"),
                                AX_X, ALU.add)
                v.tensor_reduce(first_cnt[:], first_sel[:], AX_X, ALU.add).then_inc(rank_step, 1)
                dve.wait_ge(rank_step, at + 4)
                v.tensor_scalar(over[:, :, 0], rank_sel[:, :, 0], float(CAP), FAR, ALU.is_ge, ALU.mult)
                v.tensor_tensor(place[:, :, 1], rank_sel[:, :, 1], first_cnt[:], ALU.add).then_inc(rank_step, 1)
                dve.wait_ge(rank_step, at + 5)
                v.tensor_scalar(over[:, :, 1], place[:, :, 1], float(CAP), FAR, ALU.is_ge, ALU.mult)
                v.scalar_tensor_tensor(out=slot_f[:, :, 0], in0=pick[:, 0, :], scalar=-float(CAP),
                                       in1=rank_sel[:, :, 0], op0=ALU.mult, op1=ALU.add)
                v.scalar_tensor_tensor(out=slot_f[:, :, 1], in0=pick[:, 1, :], scalar=-float(CAP),
                                       in1=rank_sel[:, :, 1], op0=ALU.mult, op1=ALU.subtract).then_inc(rank_step, 1)
                dve.wait_ge(rank_step, at + 6)
                v.tensor_scalar(slot_f[:, :, 0], slot_f[:, :, 0], float(E * CAP), None, ALU.add)
                v.tensor_scalar(slot_f[:, :, 1], slot_f[:, :, 1], float(E * CAP + CAP - 1), None, ALU.add).then_inc(rank_step, 1)
                dve.wait_ge(rank_step, at + 7)
                v.tensor_tensor(slot_f[:], slot_f[:], over[:], ALU.add).then_inc(rank_step, 1)
                dve.wait_ge(rank_step, at + 8)
                v.tensor_copy(slot_u[:], slot_f[:]).then_inc(slots_ready, 1)

            v.memset(zero_rows[:], 0.0).then_inc(memset_ready, 1)
            v.memset(pad_rows[:, :, 0:D + 1], 0.0).then_inc(memset_ready, 1)
            v.memset(pad_rows[:, :, D + 1:ROW], FAR).then_inc(memset_ready, 1)
            v.memset(count[:], 0.0).then_inc(rank_out, 1)
            v.memset(v_one[:, :, DH:DH + 1], 1.0).then_inc(memset_ready, 1)
            dve.wait_ge(memset_ready, 4)
            dve.wait_ge(rank_out, 1)
            dve.wait_ge(g_in, 32)
            dve.wait_ge(consts_ready, 2)

            dve.wait_ge(wkv_in, 16)
            v.tensor_copy(wkv_hi[:], wkv_in_sb).then_inc(w_hi_ready, 1)
            dve.wait_ge(w_hi_ready, 1)
            v.tensor_tensor(wkv_lo[:], wkv_in_sb, wkv_hi[:].bitcast(F32), ALU.subtract).then_inc(w_split, 1)
            dve.wait_ge(wq_in, 16)
            v.tensor_copy(wq_hi[:], wq_in_sb).then_inc(w_hi_ready, 1)
            dve.wait_ge(w_hi_ready, 2)
            v.tensor_tensor(wq_lo[:], wq_in_sb, wq_hi[:].bitcast(F32), ALU.subtract).then_inc(w_split, 1)

            input_norms(0)
            a_job(0, "xnT")
            a_job(0, "kv")
            q_sums(0, [0, 1, 2, 3])
            q_sums(0, [4, 5, 6, 7])
            for job in [f"qT{p}" for p in range(7)] + ["kT", "qT7"]:
                a_job(0, job)

            def run(b, has_prev, has_next):
                for p in range(PAIRS):
                    pb, pp = (b, p - 1) if p >= 1 else (b - 1, 7)
                    has_values = p >= 1 or has_prev

                    def jobs(place):
                        if has_next and p in A_JOBS:
                            for job in A_JOBS[p][place]:
                                a_job(b + 1, job)

                    if has_next:
                        q_sums(b + 1, Q_SUMS.get(p, []))
                    if has_prev and p == 3:
                        y_moments(b - 1)
                    if has_prev and p == 5:
                        x1_norms(b - 1)
                    if has_values:
                        o_norm(pb, pp, 0)
                    jobs(0)
                    if has_prev and p == 2:
                        y_copy(b - 1, 0)
                        y_copy(b - 1, 1)
                    if has_prev and p == 4:
                        x1_from_y(b - 1)
                    if has_prev and p == 5:
                        x1T_copy(b - 1)
                    if has_prev and p == 6:
                        choose(b - 1)
                    if has_prev and p == 7:
                        slots(b - 1)
                    jobs(1)
                    if has_prev and p == 2:
                        y_copy(b - 1, 2)
                    if has_values:
                        o_norm(pb, pp, 1)
                    if has_prev and p == 2:
                        y_copy(b - 1, 3)
                    if p == 0:
                        values_in(b)
                        if has_next:
                            input_norms(b + 1)
                    jobs(2)

            batches(dve, run)
            b = B - 1
            o_norm(b, 7, 0)
            o_norm(b, 7, 1)
            for it in range(NT):
                y_copy(b, it)
            y_moments(b)
            x1_from_y(b)
            x1_norms(b)
            x1T_copy(b)
            choose(b)
            slots(b)

            banks = [bank_a, bank_c]

            def xtT_copy(m, k):
                g = GROUPS * m + k
                u, r = divmod(k, GR)
                if r == 0:
                    dve.wait_ge(xt_loaded[u], 16 * (m + 1))
                    if not (isinstance(m, int) and m == 0):
                        for i in range(2):
                            dve.wait_ge(sent[i], past(16 * GT * (GR * (m - 1) + (GR * (u + 1) + 1 - i) // 2)))
                    v.tensor_copy(dest_u[u][:], xt[u][:, :, D + 1]).then_inc(dest_ready, 1)
                dve.wait_ge(xtT_ps, g + 1)
                dve.wait_ge(h_ready, past(g - 1))
                v.tensor_copy(xtT[:, k % 2, :], banks[k % 2][:, 0:GT * P]).then_inc(xtT_ready, 1)

            def weigh(m, k):
                g = GROUPS * m + k
                u, r = divmod(k, GR)
                dve.wait_ge(y2_ps, g + 1)
                dve.wait_ge(sent[k % 2], 16 * GT * (GR * m + k // 2))
                for i in range(GT):
                    t = GT * r + i
                    last = v.tensor_scalar(y_sb[:, k % 2, i, :], pv[k % 2][:, i * P:i * P + P],
                                           xt[u][:, t, D:D + 1], None, ALU.mult)
                last.then_inc(y2_ready, 1)

            xtT_copy(0, 0)

            def groups(m):
                first = isinstance(m, int) and m == 0
                final = isinstance(m, int) and m == W_ITERS - 1
                for k in range(GROUPS):
                    if k < GROUPS - 1:
                        xtT_copy(m, k + 1)
                    if k > 0:
                        weigh(m, k - 1)
                    elif not first:
                        weigh(m - 1, GROUPS - 1)
                    if k == GROUPS - 1 and not final:
                        xtT_copy(m + 1, 0)
                if final:
                    weigh(m, GROUPS - 1)

            expert_pairs(dve, groups)

            for c in range(4):
                t0 = c * 8
                dve.wait_ge(comb_loaded[c], 32)
                v.tensor_tensor(comb_a[:, t0:t0 + 8, :], comb_a[:, t0:t0 + 8, :], comb_b[:, t0:t0 + 8, :],
                                ALU.add).then_inc(comb_sum, 1)
                dve.wait_ge(comb_sum, c + 1)
                v.tensor_tensor(x1_all[:, t0:t0 + 8, :], x1_all[:, t0:t0 + 8, :], comb_a[:, t0:t0 + 8, :],
                                ALU.add).then_inc(out_ready, 1)


def kernel(L0_attn_x, L0_attn_g1, L0_attn_Wq, L0_attn_Wkv, L0_attn_Wout, L0_attn_g2, L0_ffn_w_g, L0_ffn_c_fc,
           L0_ffn_c_proj):
    import concourse.bacc as bacc
    from concourse.bass_utils import run_bass_kernel_spmd

    arrays = {
        "x": np.ascontiguousarray(L0_attn_x),
        "g1": np.ascontiguousarray(L0_attn_g1),
        "wqT": np.ascontiguousarray(np.asarray(L0_attn_Wq).T),
        "wkvT": np.ascontiguousarray(np.asarray(L0_attn_Wkv).T),
        "woT": np.ascontiguousarray(np.asarray(L0_attn_Wout).T),
        "g2": np.ascontiguousarray(L0_attn_g2),
        "w_g": np.ascontiguousarray(L0_ffn_w_g),
        "c_fc": np.ascontiguousarray(L0_ffn_c_fc),
        "c_proj": np.ascontiguousarray(L0_ffn_c_proj),
    }
    nc = bacc.Bacc("TRN2", target_bir_lowering=False, num_devices=1)
    args = [nc.dram_tensor(n, a.shape, mybir.dt.from_np(a.dtype), kind="ExternalInput").ap() for n, a in arrays.items()]
    out = nc.dram_tensor("out", arrays["x"].shape, F32, kind="ExternalOutput").ap()
    build(nc, *args, out)
    r = run_bass_kernel_spmd(nc, [arrays], core_ids=[0])
    return r.results[0]["out"]
```

```python
from contextlib import ExitStack

import numpy as np

import concourse.bass as bass
from concourse import mybir

ALU = mybir.AluOpType
ACT = mybir.ActivationFunctionType
F32 = mybir.dt.float32
BF16 = mybir.dt.bfloat16
F32R = mybir.dt.float32r
U32 = mybir.dt.uint32
I32 = mybir.dt.int32
AX_X = mybir.AxisListType.X

P = 128
TOPK = 2
EPS = 1e-5
SCALE = 16.0
CAPACITY_FACTOR = 1.25

A_JOBS = {
    1: [["xnT"], ["kv"], ["q0"]],
    2: [["q1"], ["q2"], ["q3"]],
    3: [["q4"], ["q5"], ["q6"]],
    4: [["q7"], ["qT0"], ["qT1"]],
    5: [["qT2"], ["qT3"], []],
    6: [["qT4"], ["qT5"], []],
    7: [["qT6"], ["kT"], ["qT7"]],
}
Q_SUMS = {2: [0], 3: [1, 2, 3], 4: [4, 5, 6], 5: [7]}
Q_SCALES = {3: 0, 5: 1}
ORDER = ["oT6", "oT7", "xnT", "kv", "q0", "q1", "q2", "q3", "oT0", "q4", "q5", "oT1", "q6", "oT2", "q7", "qT0", "qT1",
         "oT3", "qT2", "qT3", "x1T", "oT4", "qT4", "qT5", "oT5", "qT6", "kT", "qT7"]
FIRST_ORDER = ["xnT", "kv"] + [f"q{j}" for j in range(8)] + [f"qT{p}" for p in range(7)] + ["kT", "qT7"]
ROOT_STEPS = 8


def build(nc, x, g1, wqT, wkvT, woT, g2, w_g, c_fc, c_proj, out):
    B, N, D = x.shape
    NT = N // P
    T = B * N
    HD = wqT.shape[1]
    DH = wkvT.shape[1] // 2
    H = HD // DH
    PAIRS = H // 2
    E = w_g.shape[1]
    F = c_fc.shape[2]
    FC = F // P
    CAP = int(TOPK * CAPACITY_FACTOR * T / E)
    CAP += CAP % 2
    CT = CAP // P
    GT = 2
    GR = CT // GT
    ROW = D + 2
    FAR = 1.0e6
    TINY_Q = (1e-12 / SCALE) ** 2
    TINY_K = 1e-24
    PADS = 16
    assert D == P and DH == 64 and NT == 4 and PAIRS == 8 and CT % GT == 0 and E % 2 == 0

    x_t = x.rearrange("b (t p) d -> b p t d", p=P)
    out_t = out.rearrange("b (t p) d -> p (b t) d", p=P)
    fc_t = c_fc
    proj_t = c_proj.rearrange("e (c p) d -> e p c d", p=P)

    dispatch = nc.dram_tensor("dispatch", [E * CAP, ROW], F32, kind="Internal").ap()
    combine = nc.dram_tensor("combine", [TOPK * T, D], F32, kind="Internal").ap()
    dispatch_e = dispatch.rearrange("(e t p) r -> e p t r", e=E, p=P)
    dispatch_init = dispatch.rearrange("(p i q) r -> p i (q r)", p=P, q=4)
    combine_init = combine.rearrange("(p i q) r -> p i (q r)", p=P, q=4)
    combine_k = combine.rearrange("(k t p) d -> k p t d", k=TOPK, p=P)

    with ExitStack() as ctx:
        def sb(name, shape, dt=F32):
            return ctx.enter_context(nc.sbuf_tensor(name, shape, dt))

        def ps(name, shape, dt=F32):
            return ctx.enter_context(nc.psum_tensor(name, shape, dt))

        def sem(name):
            return ctx.enter_context(nc.semaphore(name))

        wq_hi = sb("wq_hi", [P, HD], F32R)
        wq_lo = sb("wq_lo", [P, HD], F32R)
        wkv_hi = sb("wkv_hi", [P, 2 * DH], F32R)
        wkv_lo = sb("wkv_lo", [P, 2 * DH], F32R)
        wo_sb = sb("wo_sb", [P, PAIRS, D])
        wg_sb = sb("wg_sb", [P, E])
        g1_col = sb("g1_col", [P, 1])
        g2_row = sb("g2_row", [P, D])
        ident = sb("ident", [P, P])
        before = sb("before", [P, P], BF16)
        ones = sb("ones", [P, P], BF16)
        e_down = sb("e_down", [P, NT, E])
        token_id = sb("token_id", [P, NT])
        zero_rows = sb("zero_rows", [P, 4 * D])
        pad_rows = sb("pad_rows", [P, 4, ROW])
        x_in = sb("x_in", [P, NT, D])
        ln_stats = sb("ln_stats", [P, NT, 6])
        ln_mv = sb("ln_mv", [P, NT, 2])
        ln_var = sb("ln_var", [P, NT])
        ln_tmp = sb("ln_tmp", [P, NT])
        ln_rstd = sb("ln_rstd", [P, NT])
        xn = sb("xn", [P, NT, D])
        xnT_hi = sb("xnT_hi", [P, N], F32R)
        xnT_lo = sb("xnT_lo", [P, N], F32R)
        kv_sb = sb("kv_sb", [P, NT, 2 * DH])
        k_sq = sb("k_sq", [P, NT, DH])
        k_ss = sb("k_ss", [P, NT])
        k_tmp = sb("k_tmp", [P, NT])
        k_rn = sb("k_rn", [P, NT])
        k_two = sb("k_two", [P, NT, 2, DH])
        q_tok = sb("q_tok", [P, NT, HD])
        q_sq = sb("q_sq", [P, 8, N])
        q_ss = sb("q_ss", [P, NT, 8])
        q_tmp = sb("q_tmp", [P, NT, 8])
        q_rn = sb("q_rn", [P, NT, 8])
        q_unit = sb("q_unit", [P, 2, NT, 8])
        kT_hi = sb("kT_hi", [P, N], F32R)
        kT_lo = sb("kT_lo", [P, N], F32R)
        qT = sb("qT", [P, PAIRS, 2, N], F32R)
        v_one = sb("v_one", [P, NT, DH + 1])
        probs = sb("probs", [P, 2, 2, 1280])
        rsum = sb("rsum", [P, 2, NT])
        o_tok = sb("o_tok", [P, 2, NT, 2 * DH])
        oT = sb("oT", [P, PAIRS, N])
        x_res = sb("x_res", [P, NT, D])
        y_tok = sb("y_tok", [P, NT, D])
        yn = sb("yn", [P, NT, D])
        x1_all = sb("x1_all", [P, B * NT, D])
        c_stats = sb("c_stats", [P, NT, 6])
        c_mv = sb("c_mv", [P, NT, 2])
        c_var = sb("c_var", [P, NT])
        c_tmp = sb("c_tmp", [P, NT])
        c_rstd = sb("c_rstd", [P, NT])
        rows = sb("rows", [P, NT, TOPK, ROW])
        x1T = sb("x1T", [P, N])
        logits = sb("logits", [P, NT, E])
        lg_rest = sb("lg_rest", [P, NT, E])
        eq = sb("eq", [P, NT, E])
        top = sb("top", [P, TOPK, NT])
        pick = sb("pick", [P, TOPK, NT])
        mask = sb("mask", [P, NT, TOPK, E], BF16)
        gap = sb("gap", [P, NT])
        gap_exp = sb("gap_exp", [P, NT])
        den = sb("den", [P, NT])
        w1 = sb("w1", [P, NT])
        count = sb("count", [P, TOPK, E])
        rank = sb("rank", [P, NT, TOPK, E])
        rank_sel = sb("rank_sel", [P, NT, TOPK])
        first_sel = sb("first_sel", [P, NT, E])
        first_cnt = sb("first_cnt", [P, NT])
        place = sb("place", [P, NT, TOPK])
        over = sb("over", [P, NT, TOPK])
        slot_f = sb("slot_f", [P, NT, TOPK])
        slot_u = sb("slot_u", [P, NT, TOPK], U32)
        fc_sb = [sb(f"fc_sb{u}", [P, F]) for u in range(2)]
        proj_sb = [sb(f"proj_sb{u}", [P, FC, D]) for u in range(2)]
        xt = [sb(f"xt{u}", [P, CT, ROW]) for u in range(2)]
        dest_u = [sb(f"dest_u{u}", [P, CT], U32) for u in range(2)]
        xtT = sb("xtT", [P, 2, GT * P])
        hT = sb("hT", [P, 2, FC, GT * P])
        y_sb = sb("y_sb", [P, 2, GT, D])

        hT_flat = hT[:].rearrange("p a c n -> p (a c n)")
        wq_in_sb = hT_flat[:, 0:HD]
        wkv_in_sb = hT_flat[:, HD:HD + 2 * DH]

        scores = [ps(f"scores{i}", [P, 2, 512]) for i in range(2)]
        pv = [ps(f"pv{i}", [P, 512]) for i in range(2)]
        rotating = [ps(f"rotating{i}", [P, 512]) for i in range(2)]
        pv_v = [t[:, 0:NT * (DH + 1)].rearrange("p (t d) -> p t d", t=NT) for t in pv]
        y_cols, lg_cols, rank_cols = slice(384, 384 + D), slice(384, 384 + NT * E), slice(384, 384 + (NT + 1) * TOPK * E)
        h_ps = [t[:].rearrange("p a (c n) -> p (a c) n", n=GT * P) for t in scores]

        (wq_in, wkv_in, wo_in, wg_in, g_in, init_done, x_loaded, xres_loaded,
         consts_ready, pool_const, memset_ready) = [sem(n) for n in (
            "wq_in", "wkv_in", "wo_in", "wg_in", "g_in", "init_done", "x_loaded", "xres_loaded",
            "consts_ready", "pool_const", "memset_ready")]
        (scores_ready, exp_done, masked, pv_ready, o_normed) = [sem(n) for n in (
            "scores_ready", "exp_done", "masked", "pv_ready", "o_normed")]
        (xn_ready, xnT_ps, xnT_hi_ready, xnT_ready, kv_ps, kv_out, q_ps, q_squared,
         q_summed, q_root, q_normed, k_root, k_normed, kT_ps, kT_hi_ready, kT_ready, qT_ps, qT_hi_ready, qT_ready,
         v_ready, w_hi_ready, w_split) = [sem(n) for n in (
            "xn_ready", "xnT_ps", "xnT_hi_ready", "xnT_ready", "kv_ps", "kv_out", "q_ps",
            "q_squared", "q_summed", "q_root", "q_normed", "k_root", "k_normed", "kT_ps", "kT_hi_ready", "kT_ready",
            "qT_ps", "qT_hi_ready", "qT_ready", "v_ready", "w_hi_ready", "w_split")]
        (oT_ps, oT_ready, y_ps, y_copied, y_normed, y_scaled, x1_ready, rows_ready, x1T_ps, x1T_ready, lg_ps,
         lg_ready, gap_ready, gap_exp_ready, mask_ready, rank_ps, rank_out, slots_ready, dispatched) = [sem(n) for n in (
            "oT_ps", "oT_ready", "y_ps", "y_copied", "y_normed", "y_scaled", "x1_ready", "rows_ready", "x1T_ps",
            "x1T_ready", "lg_ps", "lg_ready", "gap_ready", "gap_exp_ready", "mask_ready", "rank_ps", "rank_out",
            "slots_ready", "dispatched")]
        (ln_step, k_step, qn_step, rs_step, c_step, r_step, rank_step) = [sem(n) for n in (
            "ln_step", "k_step", "qn_step", "rs_step", "c_step", "r_step", "rank_step")]
        waits_apart = sem("waits_apart")
        w_loaded = [sem(f"w_loaded{u}") for u in range(2)]
        xt_loaded = [sem(f"xt_loaded{u}") for u in range(2)]
        (xtT_ps, xtT_ready, h_ready, gelu_done, y2_ps, y2_ready, dest_ready) = [sem(n) for n in (
            "xtT_ps", "xtT_ready", "h_ready", "gelu_done", "y2_ps", "y2_ready", "dest_ready")]
        sent = [sem(f"sent{i}") for i in range(2)]
        comb_loaded = [sem(f"comb_loaded{i}") for i in range(4)]
        (comb_sum, out_ready, stored) = [sem(n) for n in ("comb_sum", "out_ready", "stored")]

        block = ctx.enter_context(nc.Block())

        def bank(job):
            return rotating[ORDER.index(job) % 2]

        def past(n):
            return max(n, 0) if isinstance(n, int) else n

        def batches(eng, run):
            run(0, False, True)
            with eng.Fori(1, B - 1) as b:
                run(b, True, True)
            run(B - 1, True, False)

        def score_blocks(s):
            return {0: [(0, 0, 512, 0)], 1: [(1, 128, 384, 0), (3, 384, 128, 384)], 2: [(2, 256, 256, 0)]}[s]

        def prob_block(jt, it):
            return {0: it * P, 1: 512 + (it - 1) * P, 2: 1024 + (it - 2) * P, 3: 896}[jt]

        W_ITERS = E // 2
        GROUPS = 2 * GR

        def expert_pairs(eng, run):
            run(0)
            with eng.Fori(1, W_ITERS - 1) as m:
                run(m)
            run(W_ITERS - 1)

        comb_a = q_sq[:].rearrange("p a n -> p (a n)").rearrange("p (t d) -> p t d", d=D)
        comb_b = oT[:].rearrange("p a n -> p (a n)").rearrange("p (t d) -> p t d", d=D)

        @block.sync
        def _(sp):
            sp.dma_start(x_in[:], x_t[0]).then_inc(x_loaded, 16)
            sp.dma_start(wkv_in_sb, wkvT).then_inc(wkv_in, 16)
            sp.dma_start(wq_in_sb, wqT).then_inc(wq_in, 16)
            sp.dma_start(x_res[:], x_t[0]).then_inc(xres_loaded, 16)
            sp.dma_start(wo_sb[:], woT.rearrange("(c p) d -> p c d", p=P)).then_inc(wo_in, 16)
            sp.dma_start(wg_sb[:], w_g).then_inc(wg_in, 16)
            sp.wait_ge(memset_ready, 3)
            sp.dma_start(combine_init, zero_rows[:].unsqueeze(1).broadcast_to(
                [P, combine_init.shape[1], 4 * D])).then_inc(init_done, 16)

            def next_x(b):
                sp.wait_ge(xn_ready, past(b))
                sp.dma_start(x_in[:], x_t[b]).then_inc(x_loaded, 16)

            next_x(1)
            with sp.Fori(2, B) as b:
                next_x(b)
                sp.wait_ge(x1_ready, past(b - 1))
                sp.dma_start(x_res[:], x_t[b - 1]).then_inc(xres_loaded, 16)
            sp.wait_ge(x1_ready, past(B - 1))
            sp.dma_start(x_res[:], x_t[B - 1]).then_inc(xres_loaded, 16)

            def expert_loads(m, first):
                for u in range(2):
                    e = m * 2 + u
                    if not first:
                        sp.wait_ge(y2_ps, past(GROUPS * (m - 1) + GR * (u + 1)))
                    sp.dma_start(fc_sb[u][:], fc_t[e]).then_inc(w_loaded[u], 16)
                    sp.dma_start(proj_sb[u][:], proj_t[e]).then_inc(w_loaded[u], 16)
                    if first and u == 0:
                        sp.wait_ge(dispatched, PADS + 128 * B)
                    if not first:
                        sp.wait_ge(y2_ready, past(GROUPS * (m - 1) + GR * (u + 1)))
                    sp.dma_start(xt[u][:], dispatch_e[e]).then_inc(xt_loaded[u], 16)

            expert_loads(0, True)
            with sp.Fori(1, W_ITERS) as m:
                expert_loads(m, False)

            for i in range(2):
                sp.wait_ge(sent[i], 16 * GT * W_ITERS * GR)
            for c in range(4):
                t0 = c * 8
                sp.dma_start(comb_a[:, t0:t0 + 8, :], combine_k[0][:, t0:t0 + 8, :]).then_inc(comb_loaded[c], 16)
                sp.dma_start(comb_b[:, t0:t0 + 8, :], combine_k[1][:, t0:t0 + 8, :]).then_inc(comb_loaded[c], 16)
            for c in range(4):
                t0 = c * 8
                sp.wait_ge(out_ready, c + 1)
                sp.dma_start(out_t[:, t0:t0 + 8, :], x1_all[:, t0:t0 + 8, :]).then_inc(stored, 16)
            sp.wait_ge(stored, 64)

        @block.gpsimd
        def _(pool):
            nc.gpsimd.dma_start(g1_col[:], g1.rearrange("(p o) -> p o", o=1)).then_inc(g_in, 16)
            nc.gpsimd.dma_start(g2_row[:], g2.rearrange("(o d) -> o d", o=1).broadcast_to([P, D])).then_inc(g_in, 16)
            nc.gpsimd.memset(ident[:], 0.0).then_inc(pool_const, 1)
            nc.gpsimd.memset(before[:], 1.0).then_inc(pool_const, 1)
            nc.gpsimd.memset(ones[:], 1.0).then_inc(pool_const, 1)
            nc.gpsimd.iota(e_down[:], pattern=[[0, NT], [-1, E]], base=E, channel_multiplier=0,
                           allow_small_or_imprecise_dtypes=True).then_inc(pool_const, 1)
            nc.gpsimd.iota(token_id[:], pattern=[[P, NT]], base=0, channel_multiplier=1,
                           allow_small_or_imprecise_dtypes=True).then_inc(pool_const, 1)
            pool.wait_ge(pool_const, 5)
            nc.gpsimd.affine_select(out=ident[:], in_=ident[:], compare_op=ALU.not_equal, fill=1.0, base=0,
                                    pattern=[[-1, P]], channel_multiplier=1).then_inc(consts_ready, 1)
            nc.gpsimd.affine_select(out=before[:], in_=before[:], compare_op=ALU.is_gt, fill=0.0, base=0,
                                    pattern=[[1, P]], channel_multiplier=-1).then_inc(consts_ready, 1)

            def q_scale(n, half, its):
                pool.wait_ge(q_root, 2 * n + half + 1)
                for it in its:
                    q = q_tok[:, it, half * 512:half * 512 + 512].rearrange("p (h d) -> p h d", d=DH)
                    nc.gpsimd.tensor_tensor(q, q, q_unit[:, half, it, :].unsqueeze(2).broadcast_to([P, 8, DH]),
                                            ALU.mult).then_inc(q_normed, 1)

            def causal(b, p, s):
                pool.wait_ge(exp_done, 24 * b + 3 * p + s + 1)
                pool.sem_inc(waits_apart, 1)
                for jt, i0, n, c in score_blocks(s):
                    v = probs[:, p % 2, :, 512 * s + c:512 * s + c + P]
                    last = nc.gpsimd.affine_select(out=v, in_=v, compare_op=ALU.is_ge, fill=0.0, base=0,
                                                   pattern=[[0, 2], [1, P]], channel_multiplier=-1)
                last.then_inc(masked, 1)

            def dispatch_rows(b, parts):
                for i in parts:
                    if i == 0:
                        pool.wait_ge(slots_ready, b + 1)
                        pool.wait_ge(dispatched, PADS + 128 * b)
                        pool.sem_inc(waits_apart, 1)
                    k, it = 1 - i // NT, i % NT
                    pool.indirect_dma_start(
                        out=dispatch, out_offset=bass.IndirectOffsetOnAxis(ap=slot_u[:, it, k:k + 1], axis=0),
                        in_=rows[:, it, k, :], in_offset=None, bounds_check=E * CAP - 1,
                        oob_is_err=False).then_inc(dispatched, 16)

            pool.wait_ge(memset_ready, 4)
            pool.dma_start(dispatch_init, pad_rows[:].rearrange("p q r -> p (q r)").unsqueeze(1).broadcast_to(
                [P, dispatch_init.shape[1], 4 * ROW])).then_inc(dispatched, 16)
            for half in range(2):
                q_scale(0, half, range(NT))

            def run(b, has_rows, has_next):
                for p in range(PAIRS):
                    for s in range(3):
                        causal(b, p, s)
                        if has_next and p in Q_SCALES and s < 2:
                            q_scale(b + 1, Q_SCALES[p], range(2 * s, 2 * s + 2))
                        if has_rows and 3 * p + s < TOPK * NT:
                            dispatch_rows(b - 2, [3 * p + s])

            run(0, False, True)
            run(1, False, True)
            with pool.Fori(2, B - 1) as b:
                run(b, True, True)
            run(B - 1, True, False)
            dispatch_rows(B - 2, range(TOPK * NT))
            dispatch_rows(B - 1, range(TOPK * NT))

            pool.wait_ge(init_done, 16)

            def groups(m):
                for u in range(2):
                    pool.wait_ge(dest_ready, 2 * m + u + 1)
                    pool.sem_inc(waits_apart, 1)
                    for r in range(GR):
                        k = GR * u + r
                        pool.wait_ge(y2_ready, GROUPS * m + k + 1)
                        pool.sem_inc(waits_apart, 1)
                        for i in range(GT):
                            t = GT * r + i
                            pool.indirect_dma_start(
                                out=combine, out_offset=bass.IndirectOffsetOnAxis(ap=dest_u[u][:, t:t + 1], axis=0),
                                in_=y_sb[:, k % 2, i, :], in_offset=None, bounds_check=TOPK * T - 1,
                                oob_is_err=False).then_inc(sent[k % 2], 16)

            expert_pairs(pool, groups)
            for i in range(2):
                pool.wait_ge(sent[i], 16 * GT * W_ITERS * GR)

        @block.scalar
        def _(act):
            def q_copy(n, j):
                half, it = divmod(j, NT)
                act.wait_ge(q_ps, 8 * n + j + 1)
                act.wait_ge(qT_ps, past(8 * n))
                act.wait_ge(q_summed, past(8 * n))
                src = bank(f"q{j}")
                nc.scalar.copy(q_tok[:, it, half * 512:half * 512 + 512], src[:])
                nc.scalar.activation(q_sq[:, j, :], src[:], ACT.Square).then_inc(q_squared, 1)

            def qT_copy(n, p):
                act.wait_ge(qT_ps, 8 * n + p + 1)
                src = bank(f"qT{p}")
                nc.scalar.copy(qT[0:DH, p, 0, :], src[0:DH, :])
                nc.scalar.copy(qT[DH:P, p, 1, :], src[DH:P, :]).then_inc(qT_hi_ready, 1)

            def oT_copy(b, p):
                act.wait_ge(oT_ps, 8 * b + p + 1)
                if p == 0:
                    act.wait_ge(y_ps, past(NT * b))
                nc.scalar.copy(oT[:, p, :], bank(f"oT{p}")[:]).then_inc(oT_ready, 1)

            def jobs(n, p, place):
                for job in A_JOBS[p][place] if p in A_JOBS else []:
                    if job.startswith("qT"):
                        qT_copy(n, int(job[2:]))
                    elif job.startswith("q"):
                        q_copy(n, int(job[1:]))

            def exp(b, p, s):
                act.wait_ge(scores_ready, 24 * b + 3 * p + s + 1)
                act.wait_ge(pv_ready, past(16 * b + 2 * (p - 1)))
                n = (512, 512, 256)[s]
                c = 512 * s
                slot = (p + s) % 2
                nc.scalar.activation(probs[:, p % 2, :, c:c + n], scores[slot][:, :, 0:n], ACT.Exp,
                                     scale=SCALE).then_inc(exp_done, 1)

            def gap_exponential(b):
                act.wait_ge(gap_ready, b + 1)
                nc.scalar.activation(gap_exp[:], gap[:], ACT.Exp).then_inc(gap_exp_ready, 1)

            for j in range(8):
                q_copy(0, j)
            for p in range(PAIRS):
                qT_copy(0, p)

            def run(b, has_prev, has_next):
                for p in range(PAIRS):
                    exp(b, p, 0)
                    exp(b, p, 1)
                    if p < 2 and has_prev:
                        oT_copy(b - 1, p + 6)
                    if p >= 3:
                        oT_copy(b, 0 if p == 3 else p - 2)
                    if has_next:
                        jobs(b + 1, p, 0)
                    exp(b, p, 2)
                    if has_next:
                        jobs(b + 1, p, 1)
                    if p == 3:
                        oT_copy(b, 1)
                    if has_next:
                        jobs(b + 1, p, 2)
                    if p == 6 and has_prev:
                        gap_exponential(b - 1)

            batches(act, run)
            oT_copy(B - 1, 6)
            oT_copy(B - 1, 7)
            gap_exponential(B - 1)

            def groups(m):
                for k in range(GROUPS):
                    g = GROUPS * m + k
                    act.wait_ge(h_ready, g + 1)
                    act.wait_ge(y2_ps, past(g - 1))
                    nc.scalar.activation(hT[:, k % 2], h_ps[k % 2], ACT.Gelu).then_inc(gelu_done, 1)

            expert_pairs(act, groups)

        @block.tensor
        def _(pe):
            def scores_step(b, p, s):
                g = 24 * b + 3 * p + s
                pe.wait_ge(exp_done, past(g - 1))
                if s == 0:
                    pe.wait_ge(qT_ready, 8 * b + p + 1)
                    if p == 0:
                        pe.wait_ge(kT_ready, b + 1)
                slot = scores[(p + s) % 2]
                for jt, i0, n, c in score_blocks(s):
                    for k_part in (kT_hi, kT_lo):
                        for head in range(2):
                            last = nc.tensor.matmul(slot[:, head, c:c + n], k_part[:, jt * P:jt * P + P],
                                                    qT[:, p, head, i0:i0 + n], start=(k_part is kT_hi),
                                                    stop=(k_part is kT_lo))
                last.then_inc(scores_ready, 1)

            def values(b, p, head, extra=None):
                h = 16 * b + 2 * p + head
                pe.wait_ge(o_normed, past(h - 1))
                if extra is not None:
                    extra()
                pe.wait_ge(masked, 24 * b + 3 * p + 3)
                if p == 0:
                    pe.wait_ge(v_ready, b + 1)
                for it in range(NT):
                    for jt in range(it + 1):
                        c = prob_block(jt, it)
                        last = nc.tensor.matmul(pv_v[head][:, it, :], probs[:, p % 2, head, c:c + P],
                                                v_one[:, jt, :], start=(jt == 0), stop=(jt == it))
                last.then_inc(pv_ready, 1)

            def evacuated(job, n):
                for name, done in (("oT", oT_ready), ("qT", qT_ready), ("x1T", x1T_ready), ("xnT", xnT_ready),
                                   ("kv", kv_out), ("kT", kT_ready), ("q", q_squared)):
                    if job.startswith(name):
                        of_eight = name in ("oT", "qT", "q")
                        return done, (8 * n + int(job[len(name):]) + 1 if of_eight else n + 1)

            def batch_of(job, b):
                return b - 1 if job in ("oT6", "oT7", "x1T") else b if job.startswith("oT") else b + 1

            def bank_user(job, b, has_prev, has_next):
                at = ORDER.index(job)
                for other in reversed(ORDER[at % 2:at:2]):
                    if other in ("oT6", "oT7", "x1T"):
                        there = has_prev
                    else:
                        there = other.startswith("oT") or has_next
                    if there:
                        return evacuated(other, batch_of(other, b))
                return evacuated(ORDER[-2 + at % 2], b)

            def first_bank_user(job):
                before = [o for o in FIRST_ORDER[:FIRST_ORDER.index(job)] if bank(o) is bank(job)]
                return evacuated(before[-1], 0) if before else None

            def transposes_in(tile_of, dst):
                for it in range(NT):
                    last = nc.tensor.transpose(dst[:, it * P:it * P + P], tile_of(it), ident[:])
                return last

            def a_job(n, job, free):
                dst = bank(job)
                if free is not None:
                    pe.wait_ge(*free)
                if job == "xnT":
                    pe.wait_ge(xn_ready, n + 1)
                    transposes_in(lambda it: xn[:, it, :], dst).then_inc(xnT_ps, 1)
                elif job == "kv":
                    pe.wait_ge(xnT_ready, n + 1)
                    for it in range(NT):
                        tile = slice(it * P, it * P + P)
                        nc.tensor.matmul(dst[:, tile], xnT_hi[:, tile], wkv_hi[:], start=True, stop=False)
                        nc.tensor.matmul(dst[:, tile], xnT_hi[:, tile], wkv_lo[:], start=False, stop=False)
                        last = nc.tensor.matmul(dst[:, tile], xnT_lo[:, tile], wkv_hi[:], start=False, stop=True)
                    last.then_inc(kv_ps, 1)
                elif job == "kT":
                    pe.wait_ge(k_normed, n + 1)
                    transposes_in(lambda it: k_two[:, it].rearrange("p a d -> p (a d)"), dst).then_inc(kT_ps, 1)
                elif job.startswith("qT"):
                    p = int(job[2:])
                    pe.wait_ge(q_normed, 8 * n + (4 if p < 4 else 8))
                    transposes_in(lambda it: q_tok[:, it, p * P:p * P + P], dst).then_inc(qT_ps, 1)
                else:
                    half, it = divmod(int(job[1:]), NT)
                    tile, heads = slice(it * P, it * P + P), slice(half * 512, half * 512 + 512)
                    nc.tensor.matmul(dst[:], xnT_hi[:, tile], wq_hi[:, heads], start=True, stop=False)
                    nc.tensor.matmul(dst[:], xnT_hi[:, tile], wq_lo[:, heads], start=False, stop=False)
                    nc.tensor.matmul(dst[:], xnT_lo[:, tile], wq_hi[:, heads],
                                     start=False, stop=True).then_inc(q_ps, 1)

            def o_transposes(b, p, free):
                pe.wait_ge(o_normed, 16 * b + 2 * p + 2)
                pe.wait_ge(*free)
                transposes_in(lambda it: o_tok[:, p % 2, it, :], bank(f"oT{p}")).then_inc(oT_ps, 1)

            def out_projection(b, it):
                pe.wait_ge(oT_ready, 8 * b + 8)
                for c in range(PAIRS):
                    last = nc.tensor.matmul(pv[(it + 1) % 2][:, y_cols], oT[:, c, it * P:it * P + P],
                                            wo_sb[:, c, :], start=(c == 0), stop=(c == PAIRS - 1))
                last.then_inc(y_ps, 1)

            def x1_transposes(b, free):
                pe.wait_ge(rows_ready, b + 1)
                pe.wait_ge(*free)
                transposes_in(lambda it: rows[:, it, 0, 0:D], bank("x1T")).then_inc(x1T_ps, 1)

            def router(b):
                pe.wait_ge(x1T_ready, b + 1)
                for it in range(NT):
                    last = nc.tensor.matmul(pv[1][:, 384 + it * E:384 + it * E + E], x1T[:, it * P:it * P + P],
                                            wg_sb[:], start=True, stop=True)
                last.then_inc(lg_ps, 1)

            def ranks(b):
                pe.wait_ge(mask_ready, b + 1)
                W2 = TOPK * E
                m = mask[:].rearrange("p t k e -> p t (k e)")
                for it in range(NT + 1):
                    for jt in range(min(it + 1, NT)):
                        last = nc.tensor.matmul(pv[1][:, 384 + it * W2:384 + it * W2 + W2],
                                                before[:] if jt == it else ones[:], m[:, jt, :],
                                                start=(jt == 0), stop=(jt == min(it, NT - 1)))
                last.then_inc(rank_ps, 1)

            pe.wait_ge(consts_ready, 2)
            pe.wait_ge(w_split, 2)
            for job in FIRST_ORDER:
                a_job(0, job, first_bank_user(job))
            pe.wait_ge(wo_in, 16)
            pe.wait_ge(wg_in, 16)

            def run(b, has_prev, has_next):
                for p in range(PAIRS):
                    pb, pp = (b, p - 1) if p >= 1 else (b - 1, 7)
                    has_values = p >= 1 or has_prev

                    def jobs(place):
                        if has_next and p in A_JOBS:
                            for job in A_JOBS[p][place]:
                                a_job(b + 1, job, bank_user(job, b, has_prev, has_next))

                    def free(job):
                        return bank_user(job, b, has_prev, has_next)

                    scores_step(b, p, 0)
                    if p < 2 and has_prev:
                        o_transposes(b - 1, p + 6, free(f"oT{p + 6}"))
                    if p == 6 and has_prev:
                        x1_transposes(b - 1, free("x1T"))
                    if p >= 4:
                        o_transposes(b, p - 2, free(f"oT{p - 2}"))
                    scores_step(b, p, 1)
                    if has_values:
                        project = has_prev and p in (2, 3)
                        values(pb, pp, 0, (lambda: out_projection(b - 1, 2 * p - 3)) if project else None)
                    if p == 3:
                        o_transposes(b, 0, free("oT0"))
                    jobs(0)
                    scores_step(b, p, 2)
                    jobs(1)
                    if has_values:
                        extra = None
                        if has_prev:
                            extra = {1: lambda: out_projection(b - 1, 0), 2: lambda: out_projection(b - 1, 2),
                                     6: lambda: router(b - 1), 7: lambda: ranks(b - 1)}.get(p)
                        values(pb, pp, 1, extra)
                    if p == 3:
                        o_transposes(b, 1, free("oT1"))
                    jobs(2)

            batches(pe, run)
            b = B - 1
            o_transposes(b, 6, evacuated("oT5", b))
            values(b, 7, 0)
            values(b, 7, 1)
            o_transposes(b, 7, evacuated("oT4", b))
            for it in range(NT):
                if it < 2:
                    pe.wait_ge(o_normed, 16 * b + 16)
                else:
                    pe.wait_ge(y_copied, NT * b + it - 1)
                out_projection(b, it)
            x1_transposes(b, evacuated("oT6", b))
            pe.wait_ge(y_copied, NT * b + NT)
            router(b)
            ranks(b)

            banks = rotating

            def transposes(m, k):
                u, r = divmod(k, GR)
                if r == 0:
                    pe.wait_ge(xt_loaded[u], 16 * (m + 1))
                pe.wait_ge(xtT_ready, past(GROUPS * m + k - 1))
                for i in range(GT):
                    last = nc.tensor.transpose(banks[k % 2][:, i * P:i * P + P], xt[u][:, GT * r + i, 0:D], ident[:])
                last.then_inc(xtT_ps, 1)

            def up(m, k):
                u, r = divmod(k, GR)
                g = GROUPS * m + k
                if r == 0:
                    pe.wait_ge(w_loaded[u], 32 * (m + 1))
                pe.wait_ge(xtT_ready, g + 1)
                pe.wait_ge(gelu_done, past(g - 1))
                for c in range(FC):
                    last = nc.tensor.matmul(h_ps[k % 2][:, c, :], fc_sb[u][:, c * P:c * P + P], xtT[:, k % 2, :],
                                            start=True, stop=True)
                last.then_inc(h_ready, 1)

            def down(m, k):
                u = k // GR
                g = GROUPS * m + k
                pe.wait_ge(gelu_done, g + 1)
                pe.wait_ge(y2_ready, past(g - 1))
                for i in range(GT):
                    for c in range(FC):
                        last = nc.tensor.matmul(pv[k % 2][:, i * P:i * P + P], hT[:, k % 2, c, i * P:i * P + P],
                                                proj_sb[u][:, c, :], start=(c == 0), stop=(c == FC - 1))
                last.then_inc(y2_ps, 1)

            pe.wait_ge(rank_out, B + 1)
            transposes(0, 0)

            def groups(m):
                first = isinstance(m, int) and m == 0
                final = isinstance(m, int) and m == W_ITERS - 1
                for k in range(GROUPS):
                    up(m, k)
                    if k < GROUPS - 1:
                        transposes(m, k + 1)
                    elif not final:
                        transposes(m + 1, 0)
                    if k > 0:
                        down(m, k - 1)
                    elif not first:
                        down(m - 1, GROUPS - 1)
                if final:
                    down(m, GROUPS - 1)

            expert_pairs(pe, groups)

        @block.vector
        def _(dve):
            v = nc.vector

            def inverse_root(x, y, t, step, at):
                v.tensor_scalar(y.bitcast(I32), x.bitcast(I32), -0.5, 1597463007.0, ALU.mult, ALU.add).then_inc(step, 1)
                dve.wait_ge(step, at + 1)
                v.tensor_tensor(t, x, y, ALU.mult).then_inc(step, 1)
                dve.wait_ge(step, at + 2)
                v.tensor_tensor(t, t, y, ALU.mult).then_inc(step, 1)
                dve.wait_ge(step, at + 3)
                v.scalar_tensor_tensor(out=t, in0=t, scalar=-10.0 / 3.0, in1=t, op0=ALU.add, op1=ALU.mult).then_inc(step, 1)
                dve.wait_ge(step, at + 4)
                v.scalar_tensor_tensor(out=y, in0=t, scalar=5.0, in1=y, op0=ALU.add, op1=ALU.mult).then_inc(step, 1)
                dve.wait_ge(step, at + 5)
                v.tensor_tensor(t, x, y, ALU.mult).then_inc(step, 1)
                dve.wait_ge(step, at + 6)
                v.scalar_tensor_tensor(out=t, in0=t, scalar=-27.0 / 1024.0, in1=y, op0=ALU.mult,
                                       op1=ALU.mult).then_inc(step, 1)
                dve.wait_ge(step, at + 7)
                v.scalar_tensor_tensor(out=y, in0=t, scalar=0.5625, in1=y, op0=ALU.add, op1=ALU.mult).then_inc(step, 1)
                dve.wait_ge(step, at + ROOT_STEPS)

            MOMENT_STEPS = 3 + ROOT_STEPS

            def moments(src, stats, mv, var, rstd, tmp, step, at, gain=1.0, guard=EPS):
                for it in range(NT):
                    last = v.bn_stats(stats[:, it, :], src[:, it, :])
                last.then_inc(step, 1)
                dve.wait_ge(step, at + 1)
                dve.sem_inc(waits_apart, 1)
                for it in range(NT):
                    last = v.bn_aggr(mv[:, it, :], stats[:, it, :])
                last.then_inc(step, 1)
                dve.wait_ge(step, at + 2)
                v.tensor_scalar(var[:], mv[:, :, 1], gain, guard, ALU.mult, ALU.add).then_inc(step, 1)
                dve.wait_ge(step, at + 3)
                inverse_root(var[:], rstd[:], tmp[:], step, at + 3)

            def normalise(src, dst, mv, rstd, done):
                for it in range(NT):
                    last = v.tensor_scalar(dst(it), src[:, it, :], mv[:, it, 0:1], rstd[:, it:it + 1],
                                           ALU.subtract, ALU.mult)
                last.then_inc(done, 1)

            def input_norms(n):
                dve.wait_ge(x_loaded, 16 * (n + 1))
                dve.wait_ge(xnT_ps, past(n))
                moments(x_in, ln_stats, ln_mv, ln_var, ln_rstd, ln_tmp, ln_step, MOMENT_STEPS * n, 1.0 + EPS, EPS * EPS)
                normalise(x_in, lambda it: xn[:, it, :], ln_mv, ln_rstd, xn_ready)

            K_STEPS = 3 + ROOT_STEPS

            def a_job(n, job):
                if job == "xnT":
                    dve.wait_ge(xnT_ps, n + 1)
                    dve.wait_ge(q_ps, past(8 * n))
                    v.tensor_scalar(xnT_hi[:], bank(job)[:], g1_col[:, 0:1], None, ALU.mult).then_inc(xnT_hi_ready, 1)
                    dve.wait_ge(xnT_hi_ready, n + 1)
                    v.scalar_tensor_tensor(out=xnT_lo[:], in0=bank(job)[:], scalar=g1_col[:, 0:1],
                                           in1=xnT_hi[:].bitcast(F32), op0=ALU.mult,
                                           op1=ALU.subtract).then_inc(xnT_ready, 1)
                elif job == "kv":
                    dve.wait_ge(kv_ps, n + 1)
                    dve.wait_ge(kT_ps, past(n))
                    v.tensor_copy(kv_sb[:].rearrange("p t d -> p (t d)"), bank(job)[:]).then_inc(kv_out, 1)
                    dve.wait_ge(kv_out, n + 1)
                    v.tensor_tensor(k_sq[:], kv_sb[:, :, 0:DH], kv_sb[:, :, 0:DH], ALU.mult).then_inc(k_step, 1)
                    dve.wait_ge(k_step, K_STEPS * n + 1)
                    v.tensor_reduce(k_ss[:], k_sq[:], AX_X, ALU.add).then_inc(k_step, 1)
                    dve.wait_ge(k_step, K_STEPS * n + 2)
                    v.tensor_scalar(k_ss[:], k_ss[:], TINY_K, None, ALU.max).then_inc(k_step, 1)
                    dve.wait_ge(k_step, K_STEPS * n + 3)
                    inverse_root(k_ss[:], k_rn[:], k_tmp[:], k_step, K_STEPS * n + 3)
                    for a in range(2):
                        last = v.tensor_tensor(k_two[:, :, a, :], kv_sb[:, :, 0:DH],
                                               k_rn[:].unsqueeze(2).broadcast_to([P, NT, DH]), ALU.mult)
                    last.then_inc(k_normed, 1)
                elif job == "kT":
                    dve.wait_ge(kT_ps, n + 1)
                    dve.wait_ge(scores_ready, past(24 * n))
                    v.tensor_copy(kT_hi[:], bank(job)[:]).then_inc(kT_hi_ready, 1)
                    dve.wait_ge(kT_hi_ready, n + 1)
                    v.tensor_tensor(kT_lo[:], bank(job)[:], kT_hi[:].bitcast(F32), ALU.subtract).then_inc(kT_ready, 1)
                elif job.startswith("qT"):
                    p = int(job[2:])
                    dve.wait_ge(qT_hi_ready, 8 * n + p + 1)
                    v.tensor_tensor(qT[DH:P, p, 0, :], bank(job)[0:DH, :], qT[0:DH, p, 0, :].bitcast(F32), ALU.subtract)
                    v.tensor_tensor(qT[0:DH, p, 1, :], bank(job)[DH:P, :], qT[DH:P, p, 1, :].bitcast(F32),
                                    ALU.subtract).then_inc(qT_ready, 1)

            Q_STEPS = 1 + ROOT_STEPS

            def q_sums(n, js):
                for j in js:
                    dve.wait_ge(q_squared, 8 * n + j + 1)
                    v.tensor_reduce(q_ss[:, j % NT, :], q_sq[:, j, :].rearrange("p (h d) -> p h d", d=DH),
                                    AX_X, ALU.add).then_inc(q_summed, 1)
                if js and js[-1] % NT == NT - 1:
                    half = js[-1] // NT
                    at = Q_STEPS * (2 * n + half)
                    dve.wait_ge(q_summed, 8 * n + NT * (half + 1))
                    v.tensor_scalar(q_ss[:], q_ss[:], TINY_Q, None, ALU.max).then_inc(qn_step, 1)
                    dve.wait_ge(qn_step, at + 1)
                    flat = [a[:].rearrange("p t h -> p (t h)") for a in (q_ss, q_rn, q_tmp)]
                    inverse_root(*flat, qn_step, at + 1)
                    dve.wait_ge(q_normed, past(8 * n - 4 + NT * half))
                    v.tensor_copy(q_unit[:, half], q_rn[:]).then_inc(q_root, 1)

            def values_in(b):
                dve.wait_ge(pv_ready, past(16 * b))
                v.tensor_copy(v_one[:, :, 0:DH], kv_sb[:, :, DH:2 * DH]).then_inc(v_ready, 1)

            def o_norm(b, p, head):
                h = 16 * b + 2 * p + head
                dve.wait_ge(pv_ready, h + 1)
                dve.wait_ge(oT_ps, past(8 * b + p - 1))
                v.reciprocal(rsum[:, head, :].unsqueeze(2), pv_v[head][:, :, DH:DH + 1]).then_inc(rs_step, 1)
                dve.wait_ge(rs_step, h + 1)
                v.tensor_tensor(o_tok[:, p % 2, :, head * DH:head * DH + DH], pv_v[head][:, :, 0:DH],
                                rsum[:, head, :].unsqueeze(2).broadcast_to([P, NT, DH]), ALU.mult).then_inc(o_normed, 1)

            def y_copy(b, it):
                dve.wait_ge(y_ps, NT * b + it + 1)
                v.tensor_copy(y_tok[:, it, :], pv[(it + 1) % 2][:, y_cols]).then_inc(y_copied, 1)

            C_STEPS = 2 * MOMENT_STEPS

            def y_moments(b):
                dve.wait_ge(y_copied, NT * b + NT)
                moments(y_tok, c_stats, c_mv, c_var, c_rstd, c_tmp, c_step, C_STEPS * b)

            def x1_from_y(b):
                dve.wait_ge(xres_loaded, 16 * (b + 1))
                normalise(y_tok, lambda it: yn[:, it, :], c_mv, c_rstd, y_normed)
                dve.wait_ge(y_normed, b + 1)
                v.tensor_tensor(yn[:], yn[:], g2_row[:].unsqueeze(1).broadcast_to([P, NT, D]),
                                ALU.mult).then_inc(y_scaled, 1)
                dve.wait_ge(y_scaled, b + 1)
                v.tensor_tensor(yn[:], yn[:], x_res[:], ALU.add).then_inc(x1_ready, 1)
                dve.wait_ge(x1_ready, b + 1)
                moments(yn, c_stats, c_mv, c_var, c_rstd, c_tmp, c_step, C_STEPS * b + MOMENT_STEPS)

            def x1_norms(b):
                dve.wait_ge(dispatched, PADS + 128 * b)
                normalise(yn, lambda it: rows[:, it, 0, 0:D], c_mv, c_rstd, rows_ready)
                v.tensor_copy(x1_all[:, bass.ds(b * NT, NT), :], yn[:])
                dve.wait_ge(rows_ready, b + 1)
                v.tensor_copy(rows[:, :, 1, 0:D], rows[:, :, 0, 0:D])

            def x1T_copy(b):
                dve.wait_ge(x1T_ps, b + 1)
                v.tensor_copy(x1T[:], bank("x1T")[:]).then_inc(x1T_ready, 1)

            def logits_out(b):
                dve.wait_ge(lg_ps, b + 1)
                v.tensor_copy(logits[:].rearrange("p t e -> p (t e)"), pv[1][:, lg_cols]).then_inc(lg_ready, 1)

            def choose(b):
                at = 12 * b
                dve.wait_ge(lg_ready, b + 1)
                for k in range(TOPK):
                    src = logits if k == 0 else lg_rest
                    v.tensor_reduce(top[:, k, :], src[:], AX_X, ALU.max).then_inc(r_step, 1)
                    dve.wait_ge(r_step, at + 6 * k + 1)
                    v.tensor_tensor(eq[:], src[:], top[:, k, :].unsqueeze(2).broadcast_to([P, NT, E]),
                                    ALU.is_equal).then_inc(r_step, 1)
                    dve.wait_ge(r_step, at + 6 * k + 2)
                    v.tensor_tensor(eq[:], eq[:], e_down[:], ALU.mult).then_inc(r_step, 1)
                    dve.wait_ge(r_step, at + 6 * k + 3)
                    v.tensor_reduce(pick[:, k, :], eq[:], AX_X, ALU.max).then_inc(r_step, 1)
                    dve.wait_ge(r_step, at + 6 * k + 4)
                    last = v.tensor_tensor(mask[:, :, k, :], e_down[:],
                                           pick[:, k, :].unsqueeze(2).broadcast_to([P, NT, E]), ALU.is_equal)
                    if k == 0:
                        last.then_inc(r_step, 1)
                        dve.wait_ge(r_step, at + 5)
                        v.scalar_tensor_tensor(out=lg_rest[:], in0=mask[:, :, 0, :], scalar=-3.0e38,
                                               in1=logits[:], op0=ALU.mult, op1=ALU.add).then_inc(r_step, 1)
                        dve.wait_ge(r_step, at + 6)
                last.then_inc(mask_ready, 1)
                v.tensor_tensor(gap[:], top[:, 1, :], top[:, 0, :], ALU.subtract).then_inc(gap_ready, 1)
                dve.wait_ge(gap_exp_ready, b + 1)
                v.tensor_scalar(den[:], gap_exp[:], 1.0, None, ALU.add).then_inc(r_step, 1)
                dve.wait_ge(r_step, at + 11)
                v.reciprocal(w1[:], den[:]).then_inc(r_step, 1)
                dve.wait_ge(r_step, at + 12)
                v.tensor_tensor(rows[:, :, 1, D], gap_exp[:], w1[:], ALU.mult)
                v.tensor_copy(rows[:, :, 0, D], w1[:])

            def ranks_out(b):
                dve.wait_ge(rank_ps, b + 1)
                at = 8 * b
                W2 = TOPK * E
                v.tensor_tensor(rank[:].rearrange("p t k e -> p t (k e)"),
                                pv[1][:, rank_cols].rearrange("p (t w) -> p t w", t=NT + 1)[:, 0:NT, :],
                                count[:].rearrange("p k e -> p (k e)").unsqueeze(1).broadcast_to([P, NT, W2]), ALU.add)
                v.tensor_scalar(rows[:, :, 0, D + 1], token_id[:], 0.0, None, ALU.add)
                v.tensor_scalar(rows[:, :, 1, D + 1], token_id[:], float(T), None, ALU.add).then_inc(rank_step, 1)
                dve.wait_ge(rank_step, at + 1)
                v.tensor_tensor(count[:].rearrange("p k e -> p (k e)"), count[:].rearrange("p k e -> p (k e)"),
                                pv[1][:, 384 + NT * W2:384 + NT * W2 + W2], ALU.add).then_inc(rank_out, 1)

            def slots(b):
                at = 8 * b
                v.tensor_scalar(token_id[:], token_id[:], float(N), None, ALU.add)
                v.tensor_tensor(rank[:].rearrange("p t k e -> p t (k e)"), rank[:].rearrange("p t k e -> p t (k e)"),
                                mask[:].rearrange("p t k e -> p t (k e)"), ALU.mult).then_inc(rank_step, 1)
                dve.wait_ge(rank_step, at + 2)
                dve.wait_ge(rank_out, b + 2)
                v.tensor_tensor(first_sel[:], mask[:, :, 1, :],
                                count[:, 0, :].unsqueeze(1).broadcast_to([P, NT, E]), ALU.mult).then_inc(rank_step, 1)
                dve.wait_ge(rank_step, at + 3)
                v.tensor_reduce(rank_sel[:].rearrange("p t k -> p (t k)"), rank[:].rearrange("p t k e -> p (t k) e"),
                                AX_X, ALU.add)
                v.tensor_reduce(first_cnt[:], first_sel[:], AX_X, ALU.add).then_inc(rank_step, 1)
                dve.wait_ge(rank_step, at + 4)
                v.tensor_scalar(over[:, :, 0], rank_sel[:, :, 0], float(CAP), FAR, ALU.is_ge, ALU.mult)
                v.tensor_tensor(place[:, :, 1], rank_sel[:, :, 1], first_cnt[:], ALU.add).then_inc(rank_step, 1)
                dve.wait_ge(rank_step, at + 5)
                v.tensor_scalar(over[:, :, 1], place[:, :, 1], float(CAP), FAR, ALU.is_ge, ALU.mult)
                v.scalar_tensor_tensor(out=slot_f[:, :, 0], in0=pick[:, 0, :], scalar=-float(CAP),
                                       in1=rank_sel[:, :, 0], op0=ALU.mult, op1=ALU.add)
                v.scalar_tensor_tensor(out=slot_f[:, :, 1], in0=pick[:, 1, :], scalar=-float(CAP),
                                       in1=rank_sel[:, :, 1], op0=ALU.mult, op1=ALU.subtract).then_inc(rank_step, 1)
                dve.wait_ge(rank_step, at + 6)
                v.tensor_scalar(slot_f[:, :, 0], slot_f[:, :, 0], float(E * CAP), None, ALU.add)
                v.tensor_scalar(slot_f[:, :, 1], slot_f[:, :, 1], float(E * CAP + CAP - 1), None, ALU.add).then_inc(rank_step, 1)
                dve.wait_ge(rank_step, at + 7)
                v.tensor_tensor(slot_f[:], slot_f[:], over[:], ALU.add).then_inc(rank_step, 1)
                dve.wait_ge(rank_step, at + 8)
                v.tensor_copy(slot_u[:], slot_f[:]).then_inc(slots_ready, 1)

            v.memset(zero_rows[:], 0.0).then_inc(memset_ready, 1)
            v.memset(pad_rows[:, :, 0:D + 1], 0.0).then_inc(memset_ready, 1)
            v.memset(pad_rows[:, :, D + 1:ROW], FAR).then_inc(memset_ready, 1)
            v.memset(count[:], 0.0).then_inc(rank_out, 1)
            v.memset(v_one[:, :, DH:DH + 1], 1.0).then_inc(memset_ready, 1)
            dve.wait_ge(memset_ready, 4)
            dve.wait_ge(rank_out, 1)
            dve.wait_ge(g_in, 32)
            dve.wait_ge(consts_ready, 2)

            dve.wait_ge(wkv_in, 16)
            v.tensor_copy(wkv_hi[:], wkv_in_sb).then_inc(w_hi_ready, 1)
            dve.wait_ge(w_hi_ready, 1)
            v.tensor_tensor(wkv_lo[:], wkv_in_sb, wkv_hi[:].bitcast(F32), ALU.subtract).then_inc(w_split, 1)
            dve.wait_ge(wq_in, 16)
            v.tensor_copy(wq_hi[:], wq_in_sb).then_inc(w_hi_ready, 1)
            dve.wait_ge(w_hi_ready, 2)
            v.tensor_tensor(wq_lo[:], wq_in_sb, wq_hi[:].bitcast(F32), ALU.subtract).then_inc(w_split, 1)

            input_norms(0)
            a_job(0, "xnT")
            a_job(0, "kv")
            q_sums(0, [0, 1, 2, 3])
            q_sums(0, [4, 5, 6, 7])
            for job in FIRST_ORDER[10:]:
                a_job(0, job)

            def run(b, has_prev, has_next):
                for p in range(PAIRS):
                    pb, pp = (b, p - 1) if p >= 1 else (b - 1, 7)
                    has_values = p >= 1 or has_prev

                    def jobs(place):
                        if has_next and p in A_JOBS:
                            for job in A_JOBS[p][place]:
                                a_job(b + 1, job)

                    if has_next:
                        q_sums(b + 1, Q_SUMS.get(p, []))
                    if has_prev and p == 4:
                        y_moments(b - 1)
                    if has_prev and p == 5:
                        x1_norms(b - 1)
                    if has_prev and p == 6:
                        x1T_copy(b - 1)
                    if has_prev and p in (2, 3):
                        dve.wait_ge(pv_ready, 16 * pb + 2 * pp + 1)
                        y_copy(b - 1, 2 * p - 3)
                    if has_values:
                        o_norm(pb, pp, 0)
                    jobs(0)
                    if has_prev and p == 4:
                        x1_from_y(b - 1)
                    jobs(1)
                    if has_prev and p in (1, 2, 6, 7):
                        dve.wait_ge(pv_ready, 16 * pb + 2 * pp + 2)
                    if has_prev and p in (1, 2):
                        y_copy(b - 1, 2 * p - 2)
                    if has_prev and p == 6:
                        logits_out(b - 1)
                    if has_prev and p == 7:
                        ranks_out(b - 1)
                    if has_values:
                        o_norm(pb, pp, 1)
                    if has_prev and p == 6:
                        choose(b - 1)
                    if has_prev and p == 7:
                        slots(b - 1)
                    if p == 0:
                        values_in(b)
                        if has_next:
                            input_norms(b + 1)
                    jobs(2)

            batches(dve, run)
            b = B - 1
            o_norm(b, 7, 0)
            o_norm(b, 7, 1)
            for it in range(NT):
                y_copy(b, it)
            y_moments(b)
            x1_from_y(b)
            x1_norms(b)
            x1T_copy(b)
            logits_out(b)
            choose(b)
            ranks_out(b)
            slots(b)

            banks = rotating

            def xtT_copy(m, k):
                g = GROUPS * m + k
                u, r = divmod(k, GR)
                if r == 0:
                    dve.wait_ge(xt_loaded[u], 16 * (m + 1))
                    if not (isinstance(m, int) and m == 0):
                        for i in range(2):
                            dve.wait_ge(sent[i], past(16 * GT * (GR * (m - 1) + (GR * (u + 1) + 1 - i) // 2)))
                    v.tensor_copy(dest_u[u][:], xt[u][:, :, D + 1]).then_inc(dest_ready, 1)
                dve.wait_ge(xtT_ps, g + 1)
                dve.wait_ge(h_ready, past(g - 1))
                v.tensor_copy(xtT[:, k % 2, :], banks[k % 2][:, 0:GT * P]).then_inc(xtT_ready, 1)

            def weigh(m, k):
                g = GROUPS * m + k
                u, r = divmod(k, GR)
                dve.wait_ge(y2_ps, g + 1)
                dve.wait_ge(sent[k % 2], 16 * GT * (GR * m + k // 2))
                for i in range(GT):
                    t = GT * r + i
                    last = v.tensor_scalar(y_sb[:, k % 2, i, :], pv[k % 2][:, i * P:i * P + P],
                                           xt[u][:, t, D:D + 1], None, ALU.mult)
                last.then_inc(y2_ready, 1)

            xtT_copy(0, 0)

            def groups(m):
                first = isinstance(m, int) and m == 0
                final = isinstance(m, int) and m == W_ITERS - 1
                for k in range(GROUPS):
                    if k < GROUPS - 1:
                        xtT_copy(m, k + 1)
                    if k > 0:
                        weigh(m, k - 1)
                    elif not first:
                        weigh(m - 1, GROUPS - 1)
                    if k == GROUPS - 1 and not final:
                        xtT_copy(m + 1, 0)
                if final:
                    weigh(m, GROUPS - 1)

            expert_pairs(dve, groups)

            for c in range(4):
                t0 = c * 8
                dve.wait_ge(comb_loaded[c], 32)
                v.tensor_tensor(comb_a[:, t0:t0 + 8, :], comb_a[:, t0:t0 + 8, :], comb_b[:, t0:t0 + 8, :],
                                ALU.add).then_inc(comb_sum, 1)
                dve.wait_ge(comb_sum, c + 1)
                v.tensor_tensor(x1_all[:, t0:t0 + 8, :], x1_all[:, t0:t0 + 8, :], comb_a[:, t0:t0 + 8, :],
                                ALU.add).then_inc(out_ready, 1)


def kernel(L0_attn_x, L0_attn_g1, L0_attn_Wq, L0_attn_Wkv, L0_attn_Wout, L0_attn_g2, L0_ffn_w_g, L0_ffn_c_fc,
           L0_ffn_c_proj):
    import concourse.bacc as bacc
    from concourse.bass_utils import run_bass_kernel_spmd

    arrays = {
        "x": np.ascontiguousarray(L0_attn_x),
        "g1": np.ascontiguousarray(L0_attn_g1),
        "wqT": np.ascontiguousarray(np.asarray(L0_attn_Wq).T),
        "wkvT": np.ascontiguousarray(np.asarray(L0_attn_Wkv).T),
        "woT": np.ascontiguousarray(np.asarray(L0_attn_Wout).T),
        "g2": np.ascontiguousarray(L0_attn_g2),
        "w_g": np.ascontiguousarray(L0_ffn_w_g),
        "c_fc": np.ascontiguousarray(L0_ffn_c_fc),
        "c_proj": np.ascontiguousarray(L0_ffn_c_proj),
    }
    nc = bacc.Bacc("TRN2", target_bir_lowering=False, num_devices=1)
    args = [nc.dram_tensor(n, a.shape, mybir.dt.from_np(a.dtype), kind="ExternalInput").ap() for n, a in arrays.items()]
    out = nc.dram_tensor("out", arrays["x"].shape, F32, kind="ExternalOutput").ap()
    build(nc, *args, out)
    r = run_bass_kernel_spmd(nc, [arrays], core_ids=[0])
    return r.results[0]["out"]
```

```python
from contextlib import ExitStack

import numpy as np

import concourse.bass as bass
from concourse import mybir

ALU = mybir.AluOpType
ACT = mybir.ActivationFunctionType
F32 = mybir.dt.float32
BF16 = mybir.dt.bfloat16
F32R = mybir.dt.float32r
U32 = mybir.dt.uint32
I32 = mybir.dt.int32
AX_X = mybir.AxisListType.X

P = 128
TOPK = 2
EPS = 1e-5
SCALE = 16.0
CAPACITY_FACTOR = 1.25

A_JOBS = {
    0: [[], [], ["xnT"]],
    1: [["kv"], ["q0"], ["q1"]],
    2: [["q2"], ["q3"], ["q4"]],
    3: [["q5"], ["q6"], ["q7"]],
    4: [[], ["qT0"], ["qT1"]],
    5: [["qT2"], ["qT3"], []],
    6: [[], ["qT4"], ["qT5"]],
    7: [["qT6"], ["kT"], ["qT7"]],
}
Q_SUMS = {2: [0, 1, 2], 3: [3, 4], 4: [5, 6, 7]}
Q_SCALES = {3: (0, {1: [0], 2: [1]}), 4: (0, {0: [2], 1: [3]}), 5: (1, {0: [0], 1: [1], 2: [2]}), 6: (1, {0: [3]})}
ORDER = ["oT6", "xnT", "oT7", "kv", "q0", "q1", "q2", "q3", "q4", "oT0", "q5", "q6", "oT1", "q7", "oT2", "qT0", "qT1",
         "oT3", "qT2", "qT3", "oT4", "x1T", "qT4", "qT5", "oT5", "qT6", "kT", "qT7"]
FIRST_ORDER = ["xnT", "kv"] + [f"q{j}" for j in range(8)] + [f"qT{p}" for p in range(7)] + ["kT", "qT7"]
ROOT_STEPS = 8


def build(nc, x, g1, wqT, wkvT, woT, g2, w_g, c_fc, c_proj, out):
    B, N, D = x.shape
    NT = N // P
    T = B * N
    HD = wqT.shape[1]
    DH = wkvT.shape[1] // 2
    H = HD // DH
    PAIRS = H // 2
    E = w_g.shape[1]
    F = c_fc.shape[2]
    FC = F // P
    CAP = int(TOPK * CAPACITY_FACTOR * T / E)
    CAP += CAP % 2
    CT = CAP // P
    GT = 2
    GR = CT // GT
    ROW = D + 2
    FAR = 1.0e6
    TINY_Q = (1e-12 / SCALE) ** 2
    TINY_K = 1e-24
    PADS = 16
    OUT_PARTS = 8
    PT = B * NT // OUT_PARTS
    assert D == P and DH == 64 and NT == 4 and PAIRS == 8 and CT % GT == 0 and E % 2 == 0

    x_t = x.rearrange("b (t p) d -> b p t d", p=P)
    out_t = out.rearrange("b (t p) d -> p (b t) d", p=P)
    fc_t = c_fc
    proj_t = c_proj.rearrange("e (c p) d -> e p c d", p=P)

    dispatch = nc.dram_tensor("dispatch", [E * CAP, ROW], F32, kind="Internal").ap()
    combine = nc.dram_tensor("combine", [TOPK * T, D], F32, kind="Internal").ap()
    dispatch_e = dispatch.rearrange("(e t p) r -> e p t r", e=E, p=P)
    dispatch_init = dispatch.rearrange("(p i q) r -> p i (q r)", p=P, q=4)
    combine_init = combine.rearrange("(p i q) r -> p i (q r)", p=P, q=4)
    combine_k = combine.rearrange("(k t p) d -> k p t d", k=TOPK, p=P)

    with ExitStack() as ctx:
        def sb(name, shape, dt=F32):
            return ctx.enter_context(nc.sbuf_tensor(name, shape, dt))

        def ps(name, shape, dt=F32):
            return ctx.enter_context(nc.psum_tensor(name, shape, dt))

        def sem(name):
            return ctx.enter_context(nc.semaphore(name))

        wq_hi = sb("wq_hi", [P, HD], F32R)
        wq_lo = sb("wq_lo", [P, HD], F32R)
        wkv_hi = sb("wkv_hi", [P, 2 * DH], F32R)
        wkv_lo = sb("wkv_lo", [P, 2 * DH], F32R)
        wo_sb = sb("wo_sb", [P, PAIRS, D])
        wg_sb = sb("wg_sb", [P, E])
        g1_col = sb("g1_col", [P, 1])
        g2_row = sb("g2_row", [P, D])
        ident = sb("ident", [P, P])
        before = sb("before", [P, P], BF16)
        ones = sb("ones", [P, P], BF16)
        e_down = sb("e_down", [P, NT, E])
        token_id = sb("token_id", [P, NT])
        zero_rows = sb("zero_rows", [P, 4 * D])
        pad_rows = sb("pad_rows", [P, 4, ROW])
        x_in = sb("x_in", [P, NT, D])
        ln_stats = sb("ln_stats", [P, NT, 6])
        ln_mv = sb("ln_mv", [P, NT, 2])
        ln_var = sb("ln_var", [P, NT])
        ln_tmp = sb("ln_tmp", [P, NT])
        ln_rstd = sb("ln_rstd", [P, NT])
        xn = sb("xn", [P, NT, D])
        xnT_hi = sb("xnT_hi", [P, N], F32R)
        xnT_lo = sb("xnT_lo", [P, N], F32R)
        kv_sb = sb("kv_sb", [P, NT, 2 * DH])
        k_sq = sb("k_sq", [P, NT, DH])
        k_ss = sb("k_ss", [P, NT])
        k_rn = sb("k_rn", [P, NT])
        k_two = sb("k_two", [P, NT, 2, DH])
        q_tok = sb("q_tok", [P, NT, HD])
        q_sq = sb("q_sq", [P, 8, N])
        q_ss = sb("q_ss", [P, 2, NT, 8])
        q_tmp = sb("q_tmp", [P, NT, 8])
        minus_half = sb("minus_half", [P, NT])
        q_unit = sb("q_unit", [P, 2, NT, 8])
        kT_hi = sb("kT_hi", [P, N], F32R)
        kT_lo = sb("kT_lo", [P, N], F32R)
        qT = sb("qT", [P, PAIRS, 2, N], F32R)
        v_one = sb("v_one", [P, NT, DH + 1])
        probs = sb("probs", [P, 2, 2, 1280])
        rsum = sb("rsum", [P, 2, NT])
        o_tok = sb("o_tok", [P, 2, NT, 2 * DH])
        oT = sb("oT", [P, PAIRS, N])
        x_res = sb("x_res", [P, NT, D])
        y_tok = sb("y_tok", [P, NT, D])
        yn = sb("yn", [P, NT, D])
        x1_all = sb("x1_all", [P, B * NT, D])
        c_stats = sb("c_stats", [P, NT, 6])
        c_mv = sb("c_mv", [P, NT, 2])
        c_var = sb("c_var", [P, NT])
        c_tmp = sb("c_tmp", [P, NT])
        c_rstd = sb("c_rstd", [P, NT])
        rows = sb("rows", [P, NT, TOPK, ROW])
        x1T = sb("x1T", [P, N])
        logits = sb("logits", [P, NT, E])
        lg_rest = sb("lg_rest", [P, NT, E])
        eq = sb("eq", [P, NT, E])
        top = sb("top", [P, TOPK, NT])
        pick = sb("pick", [P, TOPK, NT])
        mask = sb("mask", [P, NT, TOPK, E], BF16)
        gap = sb("gap", [P, NT])
        gap_exp = sb("gap_exp", [P, NT])
        den = sb("den", [P, NT])
        w1 = sb("w1", [P, NT])
        count = sb("count", [P, TOPK, E])
        rank = sb("rank", [P, NT, TOPK, E])
        rank_sel = sb("rank_sel", [P, NT, TOPK])
        first_sel = sb("first_sel", [P, NT, E])
        first_cnt = sb("first_cnt", [P, NT])
        place = sb("place", [P, NT, TOPK])
        over = sb("over", [P, NT, TOPK])
        slot_f = sb("slot_f", [P, NT, TOPK])
        slot_u = sb("slot_u", [P, NT, TOPK], U32)
        fc_sb = [sb(f"fc_sb{u}", [P, F]) for u in range(2)]
        proj_sb = [sb(f"proj_sb{u}", [P, FC, D]) for u in range(2)]
        xt = [sb(f"xt{u}", [P, CT, ROW]) for u in range(2)]
        dest_u = [sb(f"dest_u{u}", [P, CT], U32) for u in range(2)]
        hT = sb("hT", [P, 2, FC, GT * P])
        y_sb = sb("y_sb", [P, 2, GT, D])

        hT_flat = hT[:].rearrange("p a c n -> p (a c n)")
        wq_in_sb = hT_flat[:, 0:HD]
        wkv_in_sb = hT_flat[:, HD:HD + 2 * DH]

        fc_hi = [qT[:, u, 0, 0:F] for u in range(2)]
        fc_lo = [qT[:, u, 1, 0:F] for u in range(2)]
        xtT_hi = [qT[:, 2, i, 0:GT * P] for i in range(2)]
        xtT_lo = [qT[:, 3, i, 0:GT * P] for i in range(2)]

        scores = [ps(f"scores{i}", [P, 2, 512]) for i in range(2)]
        pv = [ps(f"pv{i}", [P, 512]) for i in range(2)]
        rotating = [ps(f"rotating{i}", [P, 512]) for i in range(2)]
        pv_v = [t[:, 0:NT * (DH + 1)].rearrange("p (t d) -> p t d", t=NT) for t in pv]
        y_cols, lg_cols, rank_cols = slice(384, 384 + D), slice(384, 384 + NT * E), slice(384, 384 + (NT + 1) * TOPK * E)
        h_ps = [t[:].rearrange("p a (c n) -> p (a c) n", n=GT * P) for t in scores]

        (wq_in, wkv_in, wo_in, wg_in, g_in, init_done, x_loaded, xres_loaded,
         consts_ready, pool_const, memset_ready) = [sem(n) for n in (
            "wq_in", "wkv_in", "wo_in", "wg_in", "g_in", "init_done", "x_loaded", "xres_loaded",
            "consts_ready", "pool_const", "memset_ready")]
        (scores_ready, exp_done, masked, pv_ready, o_normed) = [sem(n) for n in (
            "scores_ready", "exp_done", "masked", "pv_ready", "o_normed")]
        (xn_ready, xnT_ps, xnT_hi_ready, xnT_ready, kv_ps, kv_out, q_ps, q_squared,
         q_summed, q_guarded, q_root, q_normed, k_guarded, k_root, k_normed, kT_ps, kT_hi_ready, kT_ready, qT_ps, qT_hi_ready, qT_ready,
         v_ready, w_hi_ready, w_split) = [sem(n) for n in (
            "xn_ready", "xnT_ps", "xnT_hi_ready", "xnT_ready", "kv_ps", "kv_out", "q_ps",
            "q_squared", "q_summed", "q_guarded", "q_root", "q_normed", "k_guarded", "k_root", "k_normed", "kT_ps",
            "kT_hi_ready", "kT_ready",
            "qT_ps", "qT_hi_ready", "qT_ready", "v_ready", "w_hi_ready", "w_split")]
        (oT_ps, oT_ready, y_ps, y_copied, y_normed, y_scaled, x1_ready, x1_kept, rows_ready, x1T_ps, x1T_ready, lg_ps,
         lg_ready, gap_ready, gap_exp_ready, mask_ready, rank_ps, rank_out, slots_ready, dispatched) = [sem(n) for n in (
            "oT_ps", "oT_ready", "y_ps", "y_copied", "y_normed", "y_scaled", "x1_ready", "x1_kept", "rows_ready", "x1T_ps",
            "x1T_ready", "lg_ps", "lg_ready", "gap_ready", "gap_exp_ready", "mask_ready", "rank_ps", "rank_out",
            "slots_ready", "dispatched")]
        (ln_step, k_step, rs_step, c_step, r_step, rank_step) = [sem(n) for n in (
            "ln_step", "k_step", "rs_step", "c_step", "r_step", "rank_step")]
        waits_apart = sem("waits_apart")
        w_loaded = [sem(f"w_loaded{u}") for u in range(2)]
        xt_loaded = [sem(f"xt_loaded{u}") for u in range(2)]
        fc_split = [sem(f"fc_split{u}") for u in range(2)]
        fc_hi_ready = [sem(f"fc_hi_ready{u}") for u in range(2)]
        (xtT_ps, xtT_hi_ready, xtT_ready, h_ready, gelu_done, y2_ps, y2_ready, dest_ready) = [sem(n) for n in (
            "xtT_ps", "xtT_hi_ready", "xtT_ready", "h_ready", "gelu_done", "y2_ps", "y2_ready", "dest_ready")]
        sent = [sem(f"sent{i}") for i in range(2)]
        comb_loaded = [sem(f"comb_loaded{i}") for i in range(OUT_PARTS)]
        (comb_sum, out_ready, stored) = [sem(n) for n in ("comb_sum", "out_ready", "stored")]

        block = ctx.enter_context(nc.Block())

        def bank(job):
            return rotating[ORDER.index(job) % 2]

        def past(n):
            return max(n, 0) if isinstance(n, int) else n

        def batches(eng, run):
            run(0, False, True)
            with eng.Fori(1, B - 1) as b:
                run(b, True, True)
            run(B - 1, True, False)

        def score_blocks(s):
            return {0: [(0, 0, 512, 0)], 1: [(1, 128, 384, 0), (3, 384, 128, 384)], 2: [(2, 256, 256, 0)]}[s]

        def prob_block(jt, it):
            return {0: it * P, 1: 512 + (it - 1) * P, 2: 1024 + (it - 2) * P, 3: 896}[jt]

        W_ITERS = E // 2
        GROUPS = 2 * GR

        def expert_pairs(eng, run):
            run(0)
            with eng.Fori(1, W_ITERS - 1) as m:
                run(m)
            run(W_ITERS - 1)

        comb_a = q_sq[:].rearrange("p a n -> p (a n)").rearrange("p (t d) -> p t d", d=D)
        comb_b = oT[:].rearrange("p a n -> p (a n)").rearrange("p (t d) -> p t d", d=D)

        @block.sync
        def _(sp):
            sp.dma_start(x_in[:], x_t[0]).then_inc(x_loaded, 16)
            sp.dma_start(wkv_in_sb, wkvT).then_inc(wkv_in, 16)
            sp.dma_start(wq_in_sb, wqT).then_inc(wq_in, 16)
            sp.dma_start(wo_sb[:], woT.rearrange("(c p) d -> p c d", p=P)).then_inc(wo_in, 16)
            sp.dma_start(wg_sb[:], w_g).then_inc(wg_in, 16)
            sp.wait_ge(memset_ready, 3)
            sp.dma_start(combine_init, zero_rows[:].unsqueeze(1).broadcast_to(
                [P, combine_init.shape[1], 4 * D])).then_inc(init_done, 16)

            def next_x(b):
                sp.wait_ge(xn_ready, past(b))
                sp.dma_start(x_in[:], x_t[b]).then_inc(x_loaded, 16)

            next_x(1)
            with sp.Fori(2, B) as b:
                next_x(b)

            def expert_loads(m, first):
                for u in range(2):
                    e = m * 2 + u
                    if not first:
                        sp.wait_ge(y2_ps, past(GROUPS * (m - 1) + GR * (u + 1)))
                    sp.dma_start(fc_sb[u][:], fc_t[e]).then_inc(w_loaded[u], 16)
                    sp.dma_start(proj_sb[u][:], proj_t[e]).then_inc(w_loaded[u], 16)
                    if first and u == 0:
                        sp.wait_ge(dispatched, PADS + 128 * B)
                    if not first:
                        sp.wait_ge(y2_ready, past(GROUPS * (m - 1) + GR * (u + 1)))
                    sp.dma_start(xt[u][:], dispatch_e[e]).then_inc(xt_loaded[u], 16)

            expert_loads(0, True)
            with sp.Fori(1, W_ITERS) as m:
                expert_loads(m, False)

            for i in range(2):
                sp.wait_ge(sent[i], 16 * GT * W_ITERS * GR)
            for c in range(OUT_PARTS):
                t0 = c * PT
                sp.dma_start(comb_a[:, t0:t0 + PT, :], combine_k[0][:, t0:t0 + PT, :]).then_inc(comb_loaded[c], 16)
                sp.dma_start(comb_b[:, t0:t0 + PT, :], combine_k[1][:, t0:t0 + PT, :]).then_inc(comb_loaded[c], 16)
            for c in range(OUT_PARTS):
                t0 = c * PT
                sp.wait_ge(out_ready, c + 1)
                sp.dma_start(out_t[:, t0:t0 + PT, :], x1_all[:, t0:t0 + PT, :]).then_inc(stored, 16)
            sp.wait_ge(stored, 16 * OUT_PARTS)

        @block.gpsimd
        def _(pool):
            nc.gpsimd.dma_start(g1_col[:], g1.rearrange("(p o) -> p o", o=1)).then_inc(g_in, 16)
            nc.gpsimd.dma_start(g2_row[:], g2.rearrange("(o d) -> o d", o=1).broadcast_to([P, D])).then_inc(g_in, 16)
            nc.gpsimd.dma_start(x_res[:], x_t[0]).then_inc(xres_loaded, 16)
            nc.gpsimd.memset(ident[:], 0.0).then_inc(pool_const, 1)
            nc.gpsimd.memset(before[:], 1.0).then_inc(pool_const, 1)
            nc.gpsimd.memset(ones[:], 1.0).then_inc(pool_const, 1)
            nc.gpsimd.iota(e_down[:], pattern=[[0, NT], [-1, E]], base=E, channel_multiplier=0,
                           allow_small_or_imprecise_dtypes=True).then_inc(pool_const, 1)
            nc.gpsimd.iota(token_id[:], pattern=[[P, NT]], base=0, channel_multiplier=1,
                           allow_small_or_imprecise_dtypes=True).then_inc(pool_const, 1)
            nc.gpsimd.memset(minus_half[:], -0.5).then_inc(pool_const, 1)
            pool.wait_ge(pool_const, 6)
            nc.gpsimd.affine_select(out=ident[:], in_=ident[:], compare_op=ALU.not_equal, fill=1.0, base=0,
                                    pattern=[[-1, P]], channel_multiplier=1).then_inc(consts_ready, 1)
            nc.gpsimd.affine_select(out=before[:], in_=before[:], compare_op=ALU.is_gt, fill=0.0, base=0,
                                    pattern=[[1, P]], channel_multiplier=-1).then_inc(consts_ready, 1)

            def keys_norm(n):
                pool.wait_ge(k_guarded, n + 1)
                nc.gpsimd.tensor_tensor(k_rn[:], k_ss[:], minus_half[:], ALU.pow).then_inc(k_root, 1)
                pool.wait_ge(k_root, n + 1)
                for a in range(2):
                    last = nc.gpsimd.tensor_tensor(k_two[:, :, a, :], kv_sb[:, :, 0:DH],
                                                   k_rn[:].unsqueeze(2).broadcast_to([P, NT, DH]), ALU.mult)
                last.then_inc(k_normed, 1)

            def keep_x1(b):
                pool.wait_ge(rows_ready, b + 1)
                nc.gpsimd.tensor_copy(x1_all[:, bass.ds(b * NT, NT), :], yn[:])
                nc.gpsimd.tensor_copy(rows[:, :, 1, 0:D], rows[:, :, 0, 0:D]).then_inc(x1_kept, 1)

            def q_scale(n, half, its):
                pool.wait_ge(q_root, ROOT_STEPS * (2 * n + half + 1))
                for it in its:
                    q = q_tok[:, it, half * 512:half * 512 + 512].rearrange("p (h d) -> p h d", d=DH)
                    nc.gpsimd.tensor_tensor(q, q, q_unit[:, half, it, :].unsqueeze(2).broadcast_to([P, 8, DH]),
                                            ALU.mult).then_inc(q_normed, 1)

            def causal(b, p, s):
                pool.wait_ge(exp_done, 24 * b + 3 * p + s + 1)
                pool.sem_inc(waits_apart, 1)
                for jt, i0, n, c in score_blocks(s):
                    v = probs[:, p % 2, :, 512 * s + c:512 * s + c + P]
                    last = nc.gpsimd.affine_select(out=v, in_=v, compare_op=ALU.is_ge, fill=0.0, base=0,
                                                   pattern=[[0, 2], [1, P]], channel_multiplier=-1)
                last.then_inc(masked, 1)

            def dispatch_rows(b, parts):
                for i in parts:
                    if i == 0:
                        pool.wait_ge(slots_ready, b + 1)
                        pool.wait_ge(x1_kept, b + 1)
                        pool.wait_ge(dispatched, PADS + 128 * b)
                        pool.sem_inc(waits_apart, 1)
                    k, it = 1 - i // NT, i % NT
                    pool.indirect_dma_start(
                        out=dispatch, out_offset=bass.IndirectOffsetOnAxis(ap=slot_u[:, it, k:k + 1], axis=0),
                        in_=rows[:, it, k, :], in_offset=None, bounds_check=E * CAP - 1,
                        oob_is_err=False).then_inc(dispatched, 16)

            pool.wait_ge(memset_ready, 4)
            pool.dma_start(dispatch_init, pad_rows[:].rearrange("p q r -> p (q r)").unsqueeze(1).broadcast_to(
                [P, dispatch_init.shape[1], 4 * ROW])).then_inc(dispatched, 16)
            keys_norm(0)
            for half in range(2):
                q_scale(0, half, range(NT))

            def run(b, has_rows, has_next):
                for p in range(PAIRS):
                    for s in range(3):
                        causal(b, p, s)
                        if has_next and p == 2 and s == 2:
                            keys_norm(b + 1)
                        if has_next and p in Q_SCALES and s in Q_SCALES[p][1]:
                            q_scale(b + 1, Q_SCALES[p][0], Q_SCALES[p][1][s])
                        if p == 6 and s == 1 and not (isinstance(b, int) and b == 0):
                            keep_x1(b - 1)
                            pool.dma_start(x_res[:], x_t[b]).then_inc(xres_loaded, 16)
                        if has_rows and 3 * p + s < TOPK * NT:
                            dispatch_rows(b - 2, [3 * p + s])

            run(0, False, True)
            run(1, False, True)
            with pool.Fori(2, B - 1) as b:
                run(b, True, True)
            run(B - 1, True, False)
            dispatch_rows(B - 2, range(TOPK * NT))
            keep_x1(B - 1)
            dispatch_rows(B - 1, range(TOPK * NT))

            pool.wait_ge(init_done, 16)

            def groups(m):
                for u in range(2):
                    pool.wait_ge(dest_ready, 2 * m + u + 1)
                    pool.sem_inc(waits_apart, 1)
                    for r in range(GR):
                        k = GR * u + r
                        pool.wait_ge(y2_ready, GROUPS * m + k + 1)
                        pool.sem_inc(waits_apart, 1)
                        for i in range(GT):
                            t = GT * r + i
                            pool.indirect_dma_start(
                                out=combine, out_offset=bass.IndirectOffsetOnAxis(ap=dest_u[u][:, t:t + 1], axis=0),
                                in_=y_sb[:, k % 2, i, :], in_offset=None, bounds_check=TOPK * T - 1,
                                oob_is_err=False).then_inc(sent[k % 2], 16)

            expert_pairs(pool, groups)
            for i in range(2):
                pool.wait_ge(sent[i], 16 * GT * W_ITERS * GR)

        @block.scalar
        def _(act):
            def q_copy(n, j):
                half, it = divmod(j, NT)
                act.wait_ge(q_ps, 8 * n + j + 1)
                act.wait_ge(qT_ps, past(8 * n))
                act.wait_ge(q_summed, past(8 * n))
                src = bank(f"q{j}")
                nc.scalar.copy(q_tok[:, it, half * 512:half * 512 + 512], src[:])
                nc.scalar.activation(q_sq[:, j, :], src[:], ACT.Square).then_inc(q_squared, 1)

            def qT_copy(n, p):
                act.wait_ge(qT_ps, 8 * n + p + 1)
                src = bank(f"qT{p}")
                nc.scalar.copy(qT[0:DH, p, 0, :], src[0:DH, :])
                nc.scalar.copy(qT[DH:P, p, 1, :], src[DH:P, :]).then_inc(qT_hi_ready, 1)

            def oT_copy(b, p):
                act.wait_ge(oT_ps, 8 * b + p + 1)
                if p == 0:
                    act.wait_ge(y_ps, past(NT * b))
                nc.scalar.copy(oT[:, p, :], bank(f"oT{p}")[:]).then_inc(oT_ready, 1)

            def jobs(n, p, place):
                for job in A_JOBS[p][place] if p in A_JOBS else []:
                    if job.startswith("qT"):
                        qT_copy(n, int(job[2:]))
                    elif job.startswith("q"):
                        q_copy(n, int(job[1:]))

            def exp(b, p, s):
                act.wait_ge(scores_ready, 24 * b + 3 * p + s + 1)
                act.wait_ge(pv_ready, past(16 * b + 2 * (p - 1)))
                n = (512, 512, 256)[s]
                c = 512 * s
                slot = (p + s) % 2
                nc.scalar.activation(probs[:, p % 2, :, c:c + n], scores[slot][:, :, 0:n], ACT.Exp,
                                     scale=SCALE).then_inc(exp_done, 1)

            def gap_exponential(b):
                act.wait_ge(gap_ready, b + 1)
                nc.scalar.activation(gap_exp[:], gap[:], ACT.Exp).then_inc(gap_exp_ready, 1)

            for j in range(8):
                q_copy(0, j)
            for p in range(PAIRS):
                qT_copy(0, p)

            def run(b, has_prev, has_next):
                for p in range(PAIRS):
                    exp(b, p, 0)
                    exp(b, p, 1)
                    if p < 2 and has_prev:
                        oT_copy(b - 1, p + 6)
                    if p >= 3:
                        oT_copy(b, 0 if p == 3 else p - 2)
                    if has_next:
                        jobs(b + 1, p, 0)
                    exp(b, p, 2)
                    if has_next:
                        jobs(b + 1, p, 1)
                    if p == 3:
                        oT_copy(b, 1)
                    if has_next:
                        jobs(b + 1, p, 2)
                    if p == 6 and has_prev:
                        gap_exponential(b - 1)

            batches(act, run)
            oT_copy(B - 1, 6)
            oT_copy(B - 1, 7)
            gap_exponential(B - 1)

            def fc_upper(m, u):
                act.wait_ge(w_loaded[u], 32 * (m + 1))
                act.wait_ge(scores_ready, 24 * B)
                act.wait_ge(h_ready, past(GROUPS * (m - 1) + GR * (u + 1)))
                nc.scalar.copy(fc_hi[u], fc_sb[u][:]).then_inc(fc_hi_ready[u], 1)

            fc_upper(0, 0)

            def groups(m):
                final = isinstance(m, int) and m == W_ITERS - 1
                for k in range(GROUPS):
                    g = GROUPS * m + k
                    if k == GR - 2:
                        fc_upper(m, 1)
                    if k == 2 * GR - 2 and not final:
                        fc_upper(m + 1, 0)
                    act.wait_ge(h_ready, g + 1)
                    act.wait_ge(y2_ps, past(g - 1))
                    nc.scalar.activation(hT[:, k % 2], h_ps[k % 2], ACT.Gelu).then_inc(gelu_done, 1)

            expert_pairs(act, groups)

        @block.tensor
        def _(pe):
            def scores_step(b, p, s):
                g = 24 * b + 3 * p + s
                pe.wait_ge(exp_done, past(g - 1))
                if s == 0:
                    pe.wait_ge(qT_ready, 8 * b + p + 1)
                    if p == 0:
                        pe.wait_ge(kT_ready, b + 1)
                slot = scores[(p + s) % 2]
                for jt, i0, n, c in score_blocks(s):
                    for k_part in (kT_hi, kT_lo):
                        for head in range(2):
                            last = nc.tensor.matmul(slot[:, head, c:c + n], k_part[:, jt * P:jt * P + P],
                                                    qT[:, p, head, i0:i0 + n], start=(k_part is kT_hi),
                                                    stop=(k_part is kT_lo))
                last.then_inc(scores_ready, 1)

            def values(b, p, head, extra=None):
                h = 16 * b + 2 * p + head
                pe.wait_ge(o_normed, past(h - 1))
                if extra is not None:
                    extra()
                pe.wait_ge(masked, 24 * b + 3 * p + 3)
                if p == 0:
                    pe.wait_ge(v_ready, b + 1)
                for it in range(NT):
                    for jt in range(it + 1):
                        c = prob_block(jt, it)
                        last = nc.tensor.matmul(pv_v[head][:, it, :], probs[:, p % 2, head, c:c + P],
                                                v_one[:, jt, :], start=(jt == 0), stop=(jt == it))
                last.then_inc(pv_ready, 1)

            def evacuated(job, n):
                for name, done in (("oT", oT_ready), ("qT", qT_ready), ("x1T", x1T_ready), ("xnT", xnT_ready),
                                   ("kv", kv_out), ("kT", kT_ready), ("q", q_squared)):
                    if job.startswith(name):
                        of_eight = name in ("oT", "qT", "q")
                        return done, (8 * n + int(job[len(name):]) + 1 if of_eight else n + 1)

            def batch_of(job, b):
                return b - 1 if job in ("oT6", "oT7", "x1T") else b if job.startswith("oT") else b + 1

            def bank_user(job, b, has_prev, has_next):
                at = ORDER.index(job)
                for other in reversed(ORDER[at % 2:at:2]):
                    if other in ("oT6", "oT7", "x1T"):
                        there = has_prev
                    else:
                        there = other.startswith("oT") or has_next
                    if there:
                        return evacuated(other, batch_of(other, b))
                return evacuated(ORDER[-2 + at % 2], b)

            def first_bank_user(job):
                before = [o for o in FIRST_ORDER[:FIRST_ORDER.index(job)] if bank(o) is bank(job)]
                return evacuated(before[-1], 0) if before else None

            def transposes_in(tile_of, dst):
                for it in range(NT):
                    last = nc.tensor.transpose(dst[:, it * P:it * P + P], tile_of(it), ident[:])
                return last

            def a_job(n, job, free):
                dst = bank(job)
                if free is not None:
                    pe.wait_ge(*free)
                if job == "xnT":
                    pe.wait_ge(xn_ready, n + 1)
                    transposes_in(lambda it: xn[:, it, :], dst).then_inc(xnT_ps, 1)
                elif job == "kv":
                    pe.wait_ge(xnT_ready, n + 1)
                    for it in range(NT):
                        tile = slice(it * P, it * P + P)
                        nc.tensor.matmul(dst[:, tile], xnT_hi[:, tile], wkv_hi[:], start=True, stop=False)
                        nc.tensor.matmul(dst[:, tile], xnT_hi[:, tile], wkv_lo[:], start=False, stop=False)
                        last = nc.tensor.matmul(dst[:, tile], xnT_lo[:, tile], wkv_hi[:], start=False, stop=True)
                    last.then_inc(kv_ps, 1)
                elif job == "kT":
                    pe.wait_ge(k_normed, n + 1)
                    transposes_in(lambda it: k_two[:, it].rearrange("p a d -> p (a d)"), dst).then_inc(kT_ps, 1)
                elif job.startswith("qT"):
                    p = int(job[2:])
                    pe.wait_ge(q_normed, 8 * n + (4 if p < 4 else 8))
                    transposes_in(lambda it: q_tok[:, it, p * P:p * P + P], dst).then_inc(qT_ps, 1)
                else:
                    half, it = divmod(int(job[1:]), NT)
                    tile, heads = slice(it * P, it * P + P), slice(half * 512, half * 512 + 512)
                    nc.tensor.matmul(dst[:], xnT_hi[:, tile], wq_hi[:, heads], start=True, stop=False)
                    nc.tensor.matmul(dst[:], xnT_hi[:, tile], wq_lo[:, heads], start=False, stop=False)
                    nc.tensor.matmul(dst[:], xnT_lo[:, tile], wq_hi[:, heads],
                                     start=False, stop=True).then_inc(q_ps, 1)

            def o_transposes(b, p, free):
                pe.wait_ge(o_normed, 16 * b + 2 * p + 2)
                pe.wait_ge(*free)
                transposes_in(lambda it: o_tok[:, p % 2, it, :], bank(f"oT{p}")).then_inc(oT_ps, 1)

            def out_projection(b, it):
                pe.wait_ge(oT_ready, 8 * b + 8)
                for c in range(PAIRS):
                    last = nc.tensor.matmul(pv[(it + 1) % 2][:, y_cols], oT[:, c, it * P:it * P + P],
                                            wo_sb[:, c, :], start=(c == 0), stop=(c == PAIRS - 1))
                last.then_inc(y_ps, 1)

            def x1_transposes(b, free):
                pe.wait_ge(rows_ready, b + 1)
                pe.wait_ge(*free)
                transposes_in(lambda it: rows[:, it, 0, 0:D], bank("x1T")).then_inc(x1T_ps, 1)

            def router(b):
                pe.wait_ge(x1T_ready, b + 1)
                for it in range(NT):
                    last = nc.tensor.matmul(pv[1][:, 384 + it * E:384 + it * E + E], x1T[:, it * P:it * P + P],
                                            wg_sb[:], start=True, stop=True)
                last.then_inc(lg_ps, 1)

            def ranks(b):
                pe.wait_ge(mask_ready, b + 1)
                W2 = TOPK * E
                m = mask[:].rearrange("p t k e -> p t (k e)")
                for it in range(NT + 1):
                    for jt in range(min(it + 1, NT)):
                        last = nc.tensor.matmul(pv[1][:, 384 + it * W2:384 + it * W2 + W2],
                                                before[:] if jt == it else ones[:], m[:, jt, :],
                                                start=(jt == 0), stop=(jt == min(it, NT - 1)))
                last.then_inc(rank_ps, 1)

            pe.wait_ge(consts_ready, 2)
            for job in FIRST_ORDER:
                if job == "kv":
                    pe.wait_ge(w_split, 2)
                a_job(0, job, first_bank_user(job))
            pe.wait_ge(wo_in, 16)
            pe.wait_ge(wg_in, 16)

            def run(b, has_prev, has_next):
                for p in range(PAIRS):
                    pb, pp = (b, p - 1) if p >= 1 else (b - 1, 7)
                    has_values = p >= 1 or has_prev

                    def jobs(place):
                        if has_next and p in A_JOBS:
                            for job in A_JOBS[p][place]:
                                a_job(b + 1, job, bank_user(job, b, has_prev, has_next))

                    def free(job):
                        return bank_user(job, b, has_prev, has_next)

                    scores_step(b, p, 0)
                    scores_step(b, p, 1)
                    if has_values:
                        project = has_prev and p in (2, 3)
                        values(pb, pp, 0, (lambda: out_projection(b - 1, 2 * p - 3)) if project else None)
                    if p < 2 and has_prev:
                        o_transposes(b - 1, p + 6, free(f"oT{p + 6}"))
                    if p == 3:
                        o_transposes(b, 0, free("oT0"))
                    if p >= 4:
                        o_transposes(b, p - 2, free(f"oT{p - 2}"))
                    if p == 6 and has_prev:
                        x1_transposes(b - 1, free("x1T"))
                    jobs(0)
                    scores_step(b, p, 2)
                    jobs(1)
                    if has_values:
                        extra = None
                        if has_prev:
                            extra = {1: lambda: out_projection(b - 1, 0), 2: lambda: out_projection(b - 1, 2),
                                     6: lambda: router(b - 1), 7: lambda: ranks(b - 1)}.get(p)
                        values(pb, pp, 1, extra)
                    if p == 3:
                        o_transposes(b, 1, free("oT1"))
                    jobs(2)

            batches(pe, run)
            b = B - 1
            o_transposes(b, 6, evacuated("oT5", b))
            values(b, 7, 0)
            values(b, 7, 1)
            o_transposes(b, 7, evacuated("oT6", b))
            for it in range(NT):
                if it < 2:
                    pe.wait_ge(o_normed, 16 * b + 16)
                else:
                    pe.wait_ge(y_copied, NT * b + it - 1)
                out_projection(b, it)
            x1_transposes(b, evacuated("oT7", b))
            pe.wait_ge(y_copied, NT * b + NT)
            router(b)
            ranks(b)

            banks = rotating

            def transposes(m, k):
                u, r = divmod(k, GR)
                if r == 0:
                    pe.wait_ge(xt_loaded[u], 16 * (m + 1))
                pe.wait_ge(xtT_ready, past(GROUPS * m + k - 1))
                for i in range(GT):
                    last = nc.tensor.transpose(banks[k % 2][:, i * P:i * P + P], xt[u][:, GT * r + i, 0:D], ident[:])
                last.then_inc(xtT_ps, 1)

            def up(m, k):
                u, r = divmod(k, GR)
                g = GROUPS * m + k
                if r == 0:
                    pe.wait_ge(fc_split[u], m + 1)
                    pe.wait_ge(w_loaded[u], 32 * (m + 1))
                pe.wait_ge(xtT_ready, g + 1)
                pe.wait_ge(gelu_done, past(g - 1))
                for c in range(FC):
                    chunk = slice(c * P, c * P + P)
                    nc.tensor.matmul(h_ps[k % 2][:, c, :], fc_hi[u][:, chunk], xtT_hi[k % 2], start=True, stop=False)
                    nc.tensor.matmul(h_ps[k % 2][:, c, :], fc_lo[u][:, chunk], xtT_hi[k % 2], start=False, stop=False)
                    last = nc.tensor.matmul(h_ps[k % 2][:, c, :], fc_hi[u][:, chunk], xtT_lo[k % 2],
                                            start=False, stop=True)
                last.then_inc(h_ready, 1)

            def down(m, k):
                u = k // GR
                g = GROUPS * m + k
                pe.wait_ge(gelu_done, g + 1)
                pe.wait_ge(y2_ready, past(g - 1))
                for i in range(GT):
                    for c in range(FC):
                        last = nc.tensor.matmul(pv[k % 2][:, i * P:i * P + P], hT[:, k % 2, c, i * P:i * P + P],
                                                proj_sb[u][:, c, :], start=(c == 0), stop=(c == FC - 1))
                last.then_inc(y2_ps, 1)

            pe.wait_ge(rank_out, B + 1)
            transposes(0, 0)

            def groups(m):
                first = isinstance(m, int) and m == 0
                final = isinstance(m, int) and m == W_ITERS - 1
                for k in range(GROUPS):
                    up(m, k)
                    if k < GROUPS - 1:
                        transposes(m, k + 1)
                    elif not final:
                        transposes(m + 1, 0)
                    if k > 0:
                        down(m, k - 1)
                    elif not first:
                        down(m - 1, GROUPS - 1)
                if final:
                    down(m, GROUPS - 1)

            expert_pairs(pe, groups)

        @block.vector
        def _(dve):
            v = nc.vector

            def inverse_root(x, y, t, step, at):
                v.tensor_scalar(y.bitcast(I32), x.bitcast(I32), -0.5, 1597463007.0, ALU.mult, ALU.add).then_inc(step, 1)
                dve.wait_ge(step, at + 1)
                v.tensor_tensor(t, x, y, ALU.mult).then_inc(step, 1)
                dve.wait_ge(step, at + 2)
                v.tensor_tensor(t, t, y, ALU.mult).then_inc(step, 1)
                dve.wait_ge(step, at + 3)
                v.scalar_tensor_tensor(out=t, in0=t, scalar=-10.0 / 3.0, in1=t, op0=ALU.add, op1=ALU.mult).then_inc(step, 1)
                dve.wait_ge(step, at + 4)
                v.scalar_tensor_tensor(out=y, in0=t, scalar=5.0, in1=y, op0=ALU.add, op1=ALU.mult).then_inc(step, 1)
                dve.wait_ge(step, at + 5)
                v.tensor_tensor(t, x, y, ALU.mult).then_inc(step, 1)
                dve.wait_ge(step, at + 6)
                v.scalar_tensor_tensor(out=t, in0=t, scalar=-27.0 / 1024.0, in1=y, op0=ALU.mult,
                                       op1=ALU.mult).then_inc(step, 1)
                dve.wait_ge(step, at + 7)
                v.scalar_tensor_tensor(out=y, in0=t, scalar=0.5625, in1=y, op0=ALU.add, op1=ALU.mult).then_inc(step, 1)
                dve.wait_ge(step, at + ROOT_STEPS)

            MOMENT_STEPS = 3 + ROOT_STEPS

            def moments(src, stats, mv, var, rstd, tmp, step, at, gain=1.0, guard=EPS):
                for it in range(NT):
                    last = v.bn_stats(stats[:, it, :], src[:, it, :])
                last.then_inc(step, 1)
                dve.wait_ge(step, at + 1)
                dve.sem_inc(waits_apart, 1)
                for it in range(NT):
                    last = v.bn_aggr(mv[:, it, :], stats[:, it, :])
                last.then_inc(step, 1)
                dve.wait_ge(step, at + 2)
                v.tensor_scalar(var[:], mv[:, :, 1], gain, guard, ALU.mult, ALU.add).then_inc(step, 1)
                dve.wait_ge(step, at + 3)
                inverse_root(var[:], rstd[:], tmp[:], step, at + 3)

            def normalise(src, dst, mv, rstd, done):
                for it in range(NT):
                    last = v.tensor_scalar(dst(it), src[:, it, :], mv[:, it, 0:1], rstd[:, it:it + 1],
                                           ALU.subtract, ALU.mult)
                last.then_inc(done, 1)

            def input_norms(n):
                dve.wait_ge(x_loaded, 16 * (n + 1))
                dve.wait_ge(xnT_ps, past(n))
                moments(x_in, ln_stats, ln_mv, ln_var, ln_rstd, ln_tmp, ln_step, MOMENT_STEPS * n, 1.0 + EPS, EPS * EPS)
                normalise(x_in, lambda it: xn[:, it, :], ln_mv, ln_rstd, xn_ready)


            def a_job(n, job):
                if job == "xnT":
                    dve.wait_ge(xnT_ps, n + 1)
                    dve.wait_ge(q_ps, past(8 * n))
                    v.tensor_scalar(xnT_hi[:], bank(job)[:], g1_col[:, 0:1], None, ALU.mult).then_inc(xnT_hi_ready, 1)
                    dve.wait_ge(xnT_hi_ready, n + 1)
                    v.scalar_tensor_tensor(out=xnT_lo[:], in0=bank(job)[:], scalar=g1_col[:, 0:1],
                                           in1=xnT_hi[:].bitcast(F32), op0=ALU.mult,
                                           op1=ALU.subtract).then_inc(xnT_ready, 1)
                elif job == "kv":
                    dve.wait_ge(kv_ps, n + 1)
                    dve.wait_ge(kT_ps, past(n))
                    v.tensor_copy(kv_sb[:].rearrange("p t d -> p (t d)"), bank(job)[:]).then_inc(kv_out, 1)
                elif job == "kT":
                    dve.wait_ge(kT_ps, n + 1)
                    dve.wait_ge(scores_ready, past(24 * n))
                    v.tensor_copy(kT_hi[:], bank(job)[:]).then_inc(kT_hi_ready, 1)
                    dve.wait_ge(kT_hi_ready, n + 1)
                    v.tensor_tensor(kT_lo[:], bank(job)[:], kT_hi[:].bitcast(F32), ALU.subtract).then_inc(kT_ready, 1)
                elif job.startswith("qT"):
                    p = int(job[2:])
                    dve.wait_ge(qT_hi_ready, 8 * n + p + 1)
                    v.tensor_tensor(qT[DH:P, p, 0, :], bank(job)[0:DH, :], qT[0:DH, p, 0, :].bitcast(F32), ALU.subtract)
                    v.tensor_tensor(qT[0:DH, p, 1, :], bank(job)[DH:P, :], qT[DH:P, p, 1, :].bitcast(F32),
                                    ALU.subtract).then_inc(qT_ready, 1)

            def key_sums(n):
                dve.wait_ge(kv_out, n + 1)
                v.tensor_tensor(k_sq[:], kv_sb[:, :, 0:DH], kv_sb[:, :, 0:DH], ALU.mult).then_inc(k_step, 1)
                dve.wait_ge(k_step, 2 * n + 1)
                v.tensor_reduce(k_ss[:], k_sq[:], AX_X, ALU.add).then_inc(k_step, 1)
                dve.wait_ge(k_step, 2 * n + 2)
                v.tensor_scalar(k_ss[:], k_ss[:], TINY_K, None, ALU.max).then_inc(k_guarded, 1)

            def q_sums(n, js):
                for j in js:
                    half, it = divmod(j, NT)
                    dve.wait_ge(q_squared, 8 * n + j + 1)
                    v.tensor_reduce(q_ss[:, half, it, :], q_sq[:, j, :].rearrange("p (h d) -> p h d", d=DH),
                                    AX_X, ALU.add).then_inc(q_summed, 1)
                    if it == NT - 1:
                        dve.wait_ge(q_summed, 8 * n + j + 1)
                        v.tensor_scalar(q_ss[:, half], q_ss[:, half], TINY_Q, None, ALU.max).then_inc(q_guarded, 1)
                        dve.wait_ge(q_guarded, 2 * n + half + 1)
                        dve.wait_ge(q_normed, past(8 * n + NT * (half - 1)))
                        flat = [a.rearrange("p t h -> p (t h)") for a in (q_ss[:, half], q_unit[:, half], q_tmp[:])]
                        inverse_root(*flat, q_root, ROOT_STEPS * (2 * n + half))

            def values_in(b):
                dve.wait_ge(pv_ready, past(16 * b))
                v.tensor_copy(v_one[:, :, 0:DH], kv_sb[:, :, DH:2 * DH]).then_inc(v_ready, 1)

            def o_norm(b, p, head):
                h = 16 * b + 2 * p + head
                dve.wait_ge(pv_ready, h + 1)
                dve.wait_ge(oT_ps, past(8 * b + p - 1))
                v.reciprocal(rsum[:, head, :].unsqueeze(2), pv_v[head][:, :, DH:DH + 1]).then_inc(rs_step, 1)
                dve.wait_ge(rs_step, h + 1)
                v.tensor_tensor(o_tok[:, p % 2, :, head * DH:head * DH + DH], pv_v[head][:, :, 0:DH],
                                rsum[:, head, :].unsqueeze(2).broadcast_to([P, NT, DH]), ALU.mult).then_inc(o_normed, 1)

            def y_copy(b, it):
                dve.wait_ge(y_ps, NT * b + it + 1)
                v.tensor_copy(y_tok[:, it, :], pv[(it + 1) % 2][:, y_cols]).then_inc(y_copied, 1)

            C_STEPS = 2 * MOMENT_STEPS

            def y_moments(b):
                dve.wait_ge(y_copied, NT * b + NT)
                moments(y_tok, c_stats, c_mv, c_var, c_rstd, c_tmp, c_step, C_STEPS * b)

            def x1_from_y(b):
                dve.wait_ge(xres_loaded, 16 * (b + 1))
                dve.wait_ge(x1_kept, past(b))
                normalise(y_tok, lambda it: yn[:, it, :], c_mv, c_rstd, y_normed)
                dve.wait_ge(y_normed, b + 1)
                v.tensor_tensor(yn[:], yn[:], g2_row[:].unsqueeze(1).broadcast_to([P, NT, D]),
                                ALU.mult).then_inc(y_scaled, 1)
                dve.wait_ge(y_scaled, b + 1)
                v.tensor_tensor(yn[:], yn[:], x_res[:], ALU.add).then_inc(x1_ready, 1)

            def x1_moments(b):
                dve.wait_ge(x1_ready, b + 1)
                moments(yn, c_stats, c_mv, c_var, c_rstd, c_tmp, c_step, C_STEPS * b + MOMENT_STEPS)

            def x1_norms(b):
                dve.wait_ge(dispatched, PADS + 128 * b)
                normalise(yn, lambda it: rows[:, it, 0, 0:D], c_mv, c_rstd, rows_ready)

            def x1T_copy(b):
                dve.wait_ge(x1T_ps, b + 1)
                v.tensor_copy(x1T[:], bank("x1T")[:]).then_inc(x1T_ready, 1)

            def logits_out(b):
                dve.wait_ge(lg_ps, b + 1)
                v.tensor_copy(logits[:].rearrange("p t e -> p (t e)"), pv[1][:, lg_cols]).then_inc(lg_ready, 1)

            def choose(b):
                at = 12 * b
                dve.wait_ge(lg_ready, b + 1)
                for k in range(TOPK):
                    src = logits if k == 0 else lg_rest
                    v.tensor_reduce(top[:, k, :], src[:], AX_X, ALU.max).then_inc(r_step, 1)
                    dve.wait_ge(r_step, at + 6 * k + 1)
                    v.tensor_tensor(eq[:], src[:], top[:, k, :].unsqueeze(2).broadcast_to([P, NT, E]),
                                    ALU.is_equal).then_inc(r_step, 1)
                    dve.wait_ge(r_step, at + 6 * k + 2)
                    v.tensor_tensor(eq[:], eq[:], e_down[:], ALU.mult).then_inc(r_step, 1)
                    dve.wait_ge(r_step, at + 6 * k + 3)
                    v.tensor_reduce(pick[:, k, :], eq[:], AX_X, ALU.max).then_inc(r_step, 1)
                    dve.wait_ge(r_step, at + 6 * k + 4)
                    last = v.tensor_tensor(mask[:, :, k, :], e_down[:],
                                           pick[:, k, :].unsqueeze(2).broadcast_to([P, NT, E]), ALU.is_equal)
                    if k == 0:
                        last.then_inc(r_step, 1)
                        dve.wait_ge(r_step, at + 5)
                        v.scalar_tensor_tensor(out=lg_rest[:], in0=mask[:, :, 0, :], scalar=-3.0e38,
                                               in1=logits[:], op0=ALU.mult, op1=ALU.add).then_inc(r_step, 1)
                        dve.wait_ge(r_step, at + 6)
                last.then_inc(mask_ready, 1)
                v.tensor_tensor(gap[:], top[:, 1, :], top[:, 0, :], ALU.subtract).then_inc(gap_ready, 1)
                dve.wait_ge(gap_exp_ready, b + 1)
                v.tensor_scalar(den[:], gap_exp[:], 1.0, None, ALU.add).then_inc(r_step, 1)
                dve.wait_ge(r_step, at + 11)
                v.reciprocal(w1[:], den[:]).then_inc(r_step, 1)
                dve.wait_ge(r_step, at + 12)
                v.tensor_tensor(rows[:, :, 1, D], gap_exp[:], w1[:], ALU.mult)
                v.tensor_copy(rows[:, :, 0, D], w1[:])

            def ranks_out(b):
                dve.wait_ge(rank_ps, b + 1)
                at = 8 * b
                W2 = TOPK * E
                v.tensor_tensor(rank[:].rearrange("p t k e -> p t (k e)"),
                                pv[1][:, rank_cols].rearrange("p (t w) -> p t w", t=NT + 1)[:, 0:NT, :],
                                count[:].rearrange("p k e -> p (k e)").unsqueeze(1).broadcast_to([P, NT, W2]), ALU.add)
                v.tensor_scalar(rows[:, :, 0, D + 1], token_id[:], 0.0, None, ALU.add)
                v.tensor_scalar(rows[:, :, 1, D + 1], token_id[:], float(T), None, ALU.add).then_inc(rank_step, 1)
                dve.wait_ge(rank_step, at + 1)
                v.tensor_tensor(count[:].rearrange("p k e -> p (k e)"), count[:].rearrange("p k e -> p (k e)"),
                                pv[1][:, 384 + NT * W2:384 + NT * W2 + W2], ALU.add).then_inc(rank_out, 1)

            def slots(b):
                at = 8 * b
                v.tensor_scalar(token_id[:], token_id[:], float(N), None, ALU.add)
                v.tensor_tensor(rank[:].rearrange("p t k e -> p t (k e)"), rank[:].rearrange("p t k e -> p t (k e)"),
                                mask[:].rearrange("p t k e -> p t (k e)"), ALU.mult).then_inc(rank_step, 1)
                dve.wait_ge(rank_step, at + 2)
                dve.wait_ge(rank_out, b + 2)
                v.tensor_tensor(first_sel[:], mask[:, :, 1, :],
                                count[:, 0, :].unsqueeze(1).broadcast_to([P, NT, E]), ALU.mult).then_inc(rank_step, 1)
                dve.wait_ge(rank_step, at + 3)
                v.tensor_reduce(rank_sel[:].rearrange("p t k -> p (t k)"), rank[:].rearrange("p t k e -> p (t k) e"),
                                AX_X, ALU.add)
                v.tensor_reduce(first_cnt[:], first_sel[:], AX_X, ALU.add).then_inc(rank_step, 1)
                dve.wait_ge(rank_step, at + 4)
                v.tensor_scalar(over[:, :, 0], rank_sel[:, :, 0], float(CAP), FAR, ALU.is_ge, ALU.mult)
                v.tensor_tensor(place[:, :, 1], rank_sel[:, :, 1], first_cnt[:], ALU.add).then_inc(rank_step, 1)
                dve.wait_ge(rank_step, at + 5)
                v.tensor_scalar(over[:, :, 1], place[:, :, 1], float(CAP), FAR, ALU.is_ge, ALU.mult)
                v.scalar_tensor_tensor(out=slot_f[:, :, 0], in0=pick[:, 0, :], scalar=-float(CAP),
                                       in1=rank_sel[:, :, 0], op0=ALU.mult, op1=ALU.add)
                v.scalar_tensor_tensor(out=slot_f[:, :, 1], in0=pick[:, 1, :], scalar=-float(CAP),
                                       in1=rank_sel[:, :, 1], op0=ALU.mult, op1=ALU.subtract).then_inc(rank_step, 1)
                dve.wait_ge(rank_step, at + 6)
                v.tensor_scalar(slot_f[:, :, 0], slot_f[:, :, 0], float(E * CAP), None, ALU.add)
                v.tensor_scalar(slot_f[:, :, 1], slot_f[:, :, 1], float(E * CAP + CAP - 1), None, ALU.add).then_inc(rank_step, 1)
                dve.wait_ge(rank_step, at + 7)
                v.tensor_tensor(slot_f[:], slot_f[:], over[:], ALU.add).then_inc(rank_step, 1)
                dve.wait_ge(rank_step, at + 8)
                v.tensor_copy(slot_u[:], slot_f[:]).then_inc(slots_ready, 1)

            v.memset(zero_rows[:], 0.0).then_inc(memset_ready, 1)
            v.memset(pad_rows[:, :, 0:D + 1], 0.0).then_inc(memset_ready, 1)
            v.memset(pad_rows[:, :, D + 1:ROW], FAR).then_inc(memset_ready, 1)
            v.memset(count[:], 0.0).then_inc(rank_out, 1)
            v.memset(v_one[:, :, DH:DH + 1], 1.0).then_inc(memset_ready, 1)
            dve.wait_ge(memset_ready, 4)
            dve.wait_ge(rank_out, 1)
            dve.wait_ge(g_in, 32)
            dve.wait_ge(consts_ready, 2)

            input_norms(0)

            dve.wait_ge(wkv_in, 16)
            v.tensor_copy(wkv_hi[:], wkv_in_sb).then_inc(w_hi_ready, 1)
            dve.wait_ge(w_hi_ready, 1)
            v.tensor_tensor(wkv_lo[:], wkv_in_sb, wkv_hi[:].bitcast(F32), ALU.subtract).then_inc(w_split, 1)
            dve.wait_ge(wq_in, 16)
            v.tensor_copy(wq_hi[:], wq_in_sb).then_inc(w_hi_ready, 1)
            dve.wait_ge(w_hi_ready, 2)
            v.tensor_tensor(wq_lo[:], wq_in_sb, wq_hi[:].bitcast(F32), ALU.subtract).then_inc(w_split, 1)

            a_job(0, "xnT")
            a_job(0, "kv")
            key_sums(0)
            q_sums(0, [0, 1, 2, 3])
            q_sums(0, [4, 5, 6, 7])
            for job in FIRST_ORDER[10:]:
                a_job(0, job)

            input_norms(1)

            def run(b, has_prev, has_next, has_next_two):
                for p in range(PAIRS):
                    pb, pp = (b, p - 1) if p >= 1 else (b - 1, 7)
                    has_values = p >= 1 or has_prev

                    def jobs(place):
                        if has_next and p in A_JOBS:
                            for job in A_JOBS[p][place]:
                                a_job(b + 1, job)

                    if has_prev and p == 6:
                        x1_norms(b - 1)
                    if has_prev and p in (2, 3):
                        dve.wait_ge(pv_ready, 16 * pb + 2 * pp + 1)
                        y_copy(b - 1, 2 * p - 3)
                    if has_values:
                        o_norm(pb, pp, 0)
                    if has_prev and p == 6:
                        x1T_copy(b - 1)
                    jobs(0)
                    if has_next:
                        q_sums(b + 1, Q_SUMS.get(p, []))
                    jobs(1)
                    if has_prev and p in (1, 2, 6, 7):
                        dve.wait_ge(pv_ready, 16 * pb + 2 * pp + 2)
                    if has_prev and p in (1, 2):
                        y_copy(b - 1, 2 * p - 2)
                    if has_prev and p == 6:
                        logits_out(b - 1)
                    if has_prev and p == 7:
                        ranks_out(b - 1)
                    if has_values:
                        o_norm(pb, pp, 1)
                    if p == 0:
                        values_in(b)
                    if p == 1 and has_next:
                        key_sums(b + 1)
                    if p == 2 and has_next_two:
                        input_norms(b + 2)
                    if has_prev and p == 3:
                        y_moments(b - 1)
                    if has_prev and p == 5:
                        x1_moments(b - 1)
                    if has_prev and p == 6:
                        choose(b - 1)
                    jobs(2)
                    if has_prev and p == 4:
                        x1_from_y(b - 1)
                    if has_prev and p == 7:
                        slots(b - 1)

            run(0, False, True, True)
            with dve.Fori(1, B - 2) as b:
                run(b, True, True, True)
            run(B - 2, True, True, False)
            run(B - 1, True, False, False)
            b = B - 1
            o_norm(b, 7, 0)
            o_norm(b, 7, 1)
            for it in range(NT):
                y_copy(b, it)
            y_moments(b)
            x1_from_y(b)
            x1_moments(b)
            x1_norms(b)
            x1T_copy(b)
            logits_out(b)
            choose(b)
            ranks_out(b)
            slots(b)

            banks = rotating

            def xtT_copy(m, k):
                g = GROUPS * m + k
                u, r = divmod(k, GR)
                if r == 0:
                    dve.wait_ge(xt_loaded[u], 16 * (m + 1))
                    if not (isinstance(m, int) and m == 0):
                        for i in range(2):
                            dve.wait_ge(sent[i], past(16 * GT * (GR * (m - 1) + (GR * (u + 1) + 1 - i) // 2)))
                    v.tensor_copy(dest_u[u][:], xt[u][:, :, D + 1]).then_inc(dest_ready, 1)
                dve.wait_ge(xtT_ps, g + 1)
                dve.wait_ge(h_ready, past(g - 1))
                v.tensor_copy(xtT_hi[k % 2], banks[k % 2][:, 0:GT * P]).then_inc(xtT_hi_ready, 1)
                dve.wait_ge(xtT_hi_ready, g + 1)
                v.tensor_tensor(xtT_lo[k % 2], banks[k % 2][:, 0:GT * P], xtT_hi[k % 2].bitcast(F32),
                                ALU.subtract).then_inc(xtT_ready, 1)

            def weigh(m, k):
                g = GROUPS * m + k
                u, r = divmod(k, GR)
                dve.wait_ge(y2_ps, g + 1)
                dve.wait_ge(sent[k % 2], 16 * GT * (GR * m + k // 2))
                for i in range(GT):
                    t = GT * r + i
                    last = v.tensor_scalar(y_sb[:, k % 2, i, :], pv[k % 2][:, i * P:i * P + P],
                                           xt[u][:, t, D:D + 1], None, ALU.mult)
                last.then_inc(y2_ready, 1)

            def fc_lower(m, u):
                dve.wait_ge(fc_hi_ready[u], m + 1)
                v.tensor_tensor(fc_lo[u], fc_sb[u][:], fc_hi[u].bitcast(F32), ALU.subtract).then_inc(fc_split[u], 1)

            fc_lower(0, 0)
            xtT_copy(0, 0)

            def groups(m):
                first = isinstance(m, int) and m == 0
                final = isinstance(m, int) and m == W_ITERS - 1
                for k in range(GROUPS):
                    if k < GROUPS - 1:
                        xtT_copy(m, k + 1)
                    elif not final:
                        xtT_copy(m + 1, 0)
                    if k > 0:
                        weigh(m, k - 1)
                    elif not first:
                        weigh(m - 1, GROUPS - 1)
                    if k == GR - 2:
                        fc_lower(m, 1)
                    if k == 2 * GR - 2 and not final:
                        fc_lower(m + 1, 0)
                if final:
                    weigh(m, GROUPS - 1)

            expert_pairs(dve, groups)

            for c in range(OUT_PARTS):
                t0 = c * PT
                dve.wait_ge(comb_loaded[c], 32)
                v.tensor_tensor(comb_a[:, t0:t0 + PT, :], comb_a[:, t0:t0 + PT, :], comb_b[:, t0:t0 + PT, :],
                                ALU.add).then_inc(comb_sum, 1)
                dve.wait_ge(comb_sum, c + 1)
                v.tensor_tensor(x1_all[:, t0:t0 + PT, :], x1_all[:, t0:t0 + PT, :], comb_a[:, t0:t0 + PT, :],
                                ALU.add).then_inc(out_ready, 1)


def kernel(L0_attn_x, L0_attn_g1, L0_attn_Wq, L0_attn_Wkv, L0_attn_Wout, L0_attn_g2, L0_ffn_w_g, L0_ffn_c_fc,
           L0_ffn_c_proj):
    import concourse.bacc as bacc
    from concourse.bass_utils import run_bass_kernel_spmd

    arrays = {
        "x": np.ascontiguousarray(L0_attn_x),
        "g1": np.ascontiguousarray(L0_attn_g1),
        "wqT": np.ascontiguousarray(np.asarray(L0_attn_Wq).T),
        "wkvT": np.ascontiguousarray(np.asarray(L0_attn_Wkv).T),
        "woT": np.ascontiguousarray(np.asarray(L0_attn_Wout).T),
        "g2": np.ascontiguousarray(L0_attn_g2),
        "w_g": np.ascontiguousarray(L0_ffn_w_g),
        "c_fc": np.ascontiguousarray(L0_ffn_c_fc),
        "c_proj": np.ascontiguousarray(L0_ffn_c_proj),
    }
    nc = bacc.Bacc("TRN2", target_bir_lowering=False, num_devices=1)
    args = [nc.dram_tensor(n, a.shape, mybir.dt.from_np(a.dtype), kind="ExternalInput").ap() for n, a in arrays.items()]
    out = nc.dram_tensor("out", arrays["x"].shape, F32, kind="ExternalOutput").ap()
    build(nc, *args, out)
    r = run_bass_kernel_spmd(nc, [arrays], core_ids=[0])
    return r.results[0]["out"]
```
